# Optimizing a Trainium2 kernel written in Bass

```python
import numpy as np
import jax
import jax.numpy as jnp

def _softmax(x, axis=-1):
    return jax.nn.softmax(x, axis=axis)

def _gelu(x):
    return jax.nn.gelu(x, approximate=True)

def _silu(x):
    return jax.nn.silu(x)

def _sigmoid(x):
    return jax.nn.sigmoid(x)

def _layernorm(x, axis=-1, eps=1e-05):
    m = jnp.mean(x, axis=axis, keepdims=True)
    v = jnp.var(x, axis=axis, keepdims=True)
    return (x - m) / jnp.sqrt(v + eps)

def _scatter_add(tgt, idx, src, axis=0):
    return tgt.at[idx].add(src)

def _segment_sum(src, seg, n):
    return jax.ops.segment_sum(src, seg, n)
kernel_name = 'mk_flamingo_gated_d1_seqx_r2_a74418'

def setup_inputs(seed: int=0):
    np.random.seed(seed)
    _w = jnp.asarray

    def _rec_inputs():
        import jax
        import jax.numpy as jnp
        _rk = jax.random.key(seed)
        x = 7.22e-05 + 1 * jax.random.normal(jax.random.fold_in(_rk, 1), (8, 224, 512), jnp.float32)
        _lenS = 224 - jax.random.randint(jax.random.fold_in(_rk, 7), (8,), 0, max(1, 224 // 4) + 1, jnp.int32)
        _lenS2 = 750 - jax.random.randint(jax.random.fold_in(_rk, 8), (8,), 0, max(1, 750 // 4) + 1, jnp.int32)
        _ctx_1024P = jax.random.normal(jax.random.fold_in(_rk, 11), (8, 16, 512), jnp.float32)
        _ctx_1024c = jax.random.dirichlet(jax.random.fold_in(_rk, 511), 0.3 * jnp.ones((16,), jnp.float32), (8, 750))
        _ctx_1024t = jnp.einsum('bsk,bkd->bsd', _ctx_1024c, _ctx_1024P)
        _ctx_1024t = _ctx_1024t * jax.lax.rsqrt(jnp.mean(jnp.square(_ctx_1024t)) + 1e-12) * 0.953939
        ctx_1024 = 4.13588e-05 + 0.999923 * (_ctx_1024t + 0.3 * jax.random.normal(jax.random.fold_in(_rk, 611), (8, 750, 512), jnp.float32))
        _g = jax.random.normal(jax.random.fold_in(_rk, 9001), (2, 1), jnp.float32)
        _g = jnp.sign(_g) * jnp.maximum(jnp.abs(_g), 1.0) + (_g == 0) * 1.0
        g_xattn = _g[0]
        g_ffn = _g[1]
        return (x, ctx_1024, g_xattn, g_ffn)
    x, ctx_1024, g_xattn, g_ffn = _rec_inputs()

    def _L0_xattn_setup():
        import jax, jax.numpy as jnp
        import numpy as np
        DIM = 512
        NUM_HEADS = 16
        HEAD_DIM = DIM // NUM_HEADS
        SCALE = HEAD_DIM ** (-0.5)

        def layer_norm(x, gamma, beta, eps=1e-05):
            mu = jnp.mean(x, axis=-1, keepdims=True)
            var = jnp.var(x, axis=-1, keepdims=True)
            return (x - mu) * jax.lax.rsqrt(var + eps) * gamma + beta
        key = jax.random.key(seed)
        ks = jax.random.split(key, 12)
        B, Nq, Nk, D = (4, 1024, 1024, DIM)
        s = D ** (-0.5)
        return {'query': jax.random.normal(ks[0], (B, Nq, D), jnp.float32), 'context': jax.random.normal(ks[1], (B, Nk, D), jnp.float32), 'Wq': jax.random.normal(ks[2], (D, D), jnp.float32) * s, 'bq': jnp.zeros((D,), jnp.float32), 'Wk': jax.random.normal(ks[3], (D, D), jnp.float32) * s, 'bk': jnp.zeros((D,), jnp.float32), 'Wv': jax.random.normal(ks[4], (D, D), jnp.float32) * s, 'bv': jnp.zeros((D,), jnp.float32), 'Wo': jax.random.normal(ks[5], (D, D), jnp.float32) * s, 'bo': jnp.zeros((D,), jnp.float32), 'gq': jnp.ones((D,), jnp.float32), 'betq': jnp.zeros((D,), jnp.float32), 'gkv': jnp.ones((D,), jnp.float32), 'betkv': jnp.zeros((D,), jnp.float32)}
    _L0_xattn_all = _L0_xattn_setup()
    _L0_xattn_in = {k: v for k, v in _L0_xattn_all.items() if k in ('Wq', 'bq', 'Wk', 'bk', 'Wv', 'bv', 'Wo', 'bo', 'gq', 'betq', 'gkv', 'betkv')}
    del _L0_xattn_all

    def _L0_ffn_setup():
        import jax, jax.numpy as jnp
        import numpy as np
        EPS = 1e-05

        def _quantize(W):
            gamma = jnp.mean(jnp.abs(W))
            return jnp.clip(jnp.round(W / (gamma + EPS)), -1.0, 1.0)
        key = jax.random.key(seed)
        k_x, k_w1, k_b1, k_w2, k_b2 = jax.random.split(key, 5)
        n_embd = 512
        d_ff = 4 * n_embd
        B, S = (4, 2048)
        bound1 = 1.0 / np.sqrt(n_embd)
        bound2 = 1.0 / np.sqrt(d_ff)
        x = jax.random.normal(k_x, (B, S, n_embd), dtype=jnp.float32)
        W1 = jax.random.uniform(k_w1, (d_ff, n_embd), jnp.float32, -bound1, bound1)
        b1 = jax.random.uniform(k_b1, (d_ff,), jnp.float32, -bound1, bound1)
        W2 = jax.random.uniform(k_w2, (n_embd, d_ff), jnp.float32, -bound2, bound2)
        b2 = jax.random.uniform(k_b2, (n_embd,), jnp.float32, -bound2, bound2)
        return {'x': x, 'W1': W1, 'b1': b1, 'W2': W2, 'b2': b2}
    _L0_ffn_all = _L0_ffn_setup()
    _L0_ffn_in = {k: v for k, v in _L0_ffn_all.items() if k in ('W1', 'b1', 'W2', 'b2')}
    del _L0_ffn_all
    return {'x': x, 'ctx_1024': ctx_1024, 'g_xattn': g_xattn, 'g_ffn': g_ffn, 'L0_xattn_Wq': _L0_xattn_in['Wq'], 'L0_xattn_bq': _L0_xattn_in['bq'], 'L0_xattn_Wk': _L0_xattn_in['Wk'], 'L0_xattn_bk': _L0_xattn_in['bk'], 'L0_xattn_Wv': _L0_xattn_in['Wv'], 'L0_xattn_bv': _L0_xattn_in['bv'], 'L0_xattn_Wo': _L0_xattn_in['Wo'], 'L0_xattn_bo': _L0_xattn_in['bo'], 'L0_xattn_gq': _L0_xattn_in['gq'], 'L0_xattn_betq': _L0_xattn_in['betq'], 'L0_xattn_gkv': _L0_xattn_in['gkv'], 'L0_xattn_betkv': _L0_xattn_in['betkv'], 'L0_ffn_W1': _L0_ffn_in['W1'], 'L0_ffn_b1': _L0_ffn_in['b1'], 'L0_ffn_W2': _L0_ffn_in['W2'], 'L0_ffn_b2': _L0_ffn_in['b2']}

def reference(x, ctx_1024, g_xattn, g_ffn, L0_xattn_Wq, L0_xattn_bq, L0_xattn_Wk, L0_xattn_bk, L0_xattn_Wv, L0_xattn_bv, L0_xattn_Wo, L0_xattn_bo, L0_xattn_gq, L0_xattn_betq, L0_xattn_gkv, L0_xattn_betkv, L0_ffn_W1, L0_ffn_b1, L0_ffn_W2, L0_ffn_b2):
    import jax
    import jax.numpy as jnp

    def _L0_xattn_ref(query, context, Wq, bq, Wk, bk, Wv, bv, Wo, bo, gq, betq, gkv, betkv):
        import jax, jax.numpy as jnp
        import numpy as np
        DIM = 512
        NUM_HEADS = 16
        HEAD_DIM = DIM // NUM_HEADS
        SCALE = HEAD_DIM ** (-0.5)

        def layer_norm(x, gamma, beta, eps=1e-05):
            mu = jnp.mean(x, axis=-1, keepdims=True)
            var = jnp.var(x, axis=-1, keepdims=True)
            return (x - mu) * jax.lax.rsqrt(var + eps) * gamma + beta
        B, Nq, D = query.shape
        H, Hd = (NUM_HEADS, HEAD_DIM)
        q = layer_norm(query, gq, betq)
        c = layer_norm(context, gkv, betkv)
        Q = (q @ Wq + bq).reshape(B, Nq, H, Hd).transpose(0, 2, 1, 3)
        K = (c @ Wk + bk).reshape(B, -1, H, Hd).transpose(0, 2, 1, 3)
        V = (c @ Wv + bv).reshape(B, -1, H, Hd).transpose(0, 2, 1, 3)
        attn = jnp.einsum('bhqd,bhkd->bhqk', Q, K) * SCALE
        attn = jax.nn.softmax(attn, axis=-1)
        out = jnp.einsum('bhqk,bhkd->bhqd', attn, V)
        out = out.transpose(0, 2, 1, 3).reshape(B, Nq, D)
        return out @ Wo + bo

    def _L0_ffn_ref(x, W1, b1, W2, b2):
        import jax, jax.numpy as jnp
        import numpy as np
        EPS = 1e-05

        def _quantize(W):
            gamma = jnp.mean(jnp.abs(W))
            return jnp.clip(jnp.round(W / (gamma + EPS)), -1.0, 1.0)
        Wq1 = _quantize(W1)
        Wq2 = _quantize(W2)
        h = jax.nn.relu(jnp.einsum('bsd,fd->bsf', x, Wq1) + b1)
        out = jnp.einsum('bsf,df->bsd', h, Wq2) + b2
        return out
    x = x + jnp.tanh(g_xattn[0]) * _L0_xattn_ref(_layernorm(x, axis=-1), ctx_1024, L0_xattn_Wq, L0_xattn_bq, L0_xattn_Wk, L0_xattn_bk, L0_xattn_Wv, L0_xattn_bv, L0_xattn_Wo, L0_xattn_bo, L0_xattn_gq, L0_xattn_betq, L0_xattn_gkv, L0_xattn_betkv)
    x = x + jnp.tanh(g_ffn[0]) * _L0_ffn_ref(_layernorm(x, axis=-1), L0_ffn_W1, L0_ffn_b1, L0_ffn_W2, L0_ffn_b2)
    return x

_drawn_inputs = setup_inputs


def setup_inputs(seed=0):
    import zlib

    import numpy as np

    out = dict(_drawn_inputs(seed))
    spreads = {'L0_xattn_bq': (0.0, 0.722),
     'L0_xattn_bk': (0.0, 2.0),
     'L0_xattn_bv': (0.0, 0.1),
     'L0_xattn_bo': (0.0, 0.1),
     'L0_xattn_gq': (1.0, 0.6),
     'L0_xattn_betq': (0.0, 0.734),
     'L0_xattn_gkv': (1.0, 0.2),
     'L0_xattn_betkv': (0.0, 0.1)}
    factors = {'L0_ffn_b1': 47.852, 'L0_ffn_b2': 64.0}
    for name, (base, spread) in spreads.items():
        noise = np.random.default_rng([zlib.crc32(name.encode()), seed]).standard_normal(out[name].shape)
        drawn = base * np.exp(spread * noise) if base else spread * noise
        out[name] = jnp.asarray(drawn.astype(out[name].dtype))
    for name, factor in factors.items():
        out[name] = (out[name] * factor).astype(out[name].dtype)
    return out
```

```python
from contextlib import ExitStack

import concourse.bass as bass
from concourse import mybir

ALU = mybir.AluOpType
ACT = mybir.ActivationFunctionType
AX = mybir.AxisListType
F32 = mybir.dt.float32
F16 = mybir.dt.float16
F8 = mybir.dt.float8e4

P = 128
B, NQ, NK, D = 8, 224, 750, 512
H, HD = 16, 32
F = 2048
DC = D // P
FC = F // P
KT, KR = 6, 125
KH = NK // 2
QSTART = (0, NQ - P)
QNEW = (0, 2 * P - NQ)
EPS = 1e-5
SPLIT_ROWS = 3 * HD
STACK_ROWS = SPLIT_ROWS + 2
VW = HD + 1

Z_SCALE, W_SCALE, Y_SCALE = 16.0, 64.0, 4.0
QK_SCALE, V_SCALE, M_SCALE = 4.0, 16.0, 16.0
PSUM_TO_QK = QK_SCALE / (Z_SCALE * W_SCALE)
PSUM_TO_V = V_SCALE / (Z_SCALE * W_SCALE)
PSUM_TO_O = 1.0 / (V_SCALE * W_SCALE)
EXP_SCALE = HD ** -0.5 / (QK_SCALE * QK_SCALE)
P_LOG_SCALE = 8.317766166719343
MAX_SHIFT = P_LOG_SCALE / EXP_SCALE / M_SCALE

PREP, FINISH, ATTEND = ("cx", "xx", "q", "k", "v"), ("ot", "op", "yt", "f1", "f2"), ("mr",)
SLOT_FILLS = [
    [],
    [("mr", 1), ("ot", 0), ("ot", 1)],
    [("op", 0), ("op", 1)],
    [("mr", 2)],
    [("yt", 0), ("yt", 1), ("xx", 0), ("xx", 1), ("cx", 0)],
    [("mr", 3), ("cx", 1), ("cx", 2), ("cx", 3), ("cx", 4), ("cx", 5)],
    [("q", 0), ("q", 1), ("f1", 0)],
    [("mr", 4), ("k", 0), ("k", 1), ("f1", 1)],
    [("k", 2), ("k", 3), ("f1", 2)],
    [("mr", 5), ("k", 4), ("k", 5), ("f1", 3)],
    [("k", 6), ("k", 7), ("f1", 4)],
    [("mr", 6), ("v", 0), ("f1", 5), ("f1", 6)],
    [("v", 1), ("f1", 7), ("v", 2)],
    [("mr", 7), ("v", 3), ("v", 4)],
    [("v", 5), ("f2", 0)],
    [("f2", 1), ("mr", -1), ("f2", 2), ("f2", 3)],
]
PIECES = 16
PIECE_RING = 3


def slot_steps(slot, attend, prep, finish):
    fills = [(k, i) for k, i in SLOT_FILLS[slot]
             if (prep and (k in PREP or i == -1)) or (finish and k in FINISH)
             or (attend and k == "mr" and i > 0)]
    early = prep if slot >= 12 else attend
    pv = attend if slot else finish
    fills = fills + [None] * 3
    steps = [("score", 0)] * early + [("expo", 0)] * attend + [fills[0]]
    steps += [("expo", 1)] * attend + [("score", 1)] * early + [fills[1]]
    steps += [("expo", 2)] * attend + [("pv", (slot - 1) % H)] * pv + fills[2:]
    return [s for s in steps if s]


FILL_KINDS = PREP + FINISH + ATTEND


def fill_list(stages):
    return [s for slot in range(H) for s in slot_steps(slot, *stages) if s[0] in FILL_KINDS]


FIRST, SECOND, INNER, LAST, TAIL = (0, 1, 0), (1, 1, 0), (1, 1, 1), (1, 0, 1), (0, 0, 1)
N_FIRST, N_SECOND, N_INNER, N_LAST = (len(fill_list(s)) for s in (FIRST, SECOND, INNER, LAST))


def fills_before(b):
    if isinstance(b, int):
        return {-1: 0, 0: N_FIRST, 7: N_FIRST + N_SECOND + 6 * N_INNER,
                8: N_FIRST + N_SECOND + 6 * N_INNER + N_LAST}[b]
    return b * N_INNER + (N_FIRST + N_SECOND - N_INNER)


def gated_block(nc, x, ctx_in, w_q, w_k, w_v, w_o, w1t, w2t, cols, bo, b2, g_x, g_f, out):
    with ExitStack() as ctx:
        def sb(name, shape, dt):
            return ctx.enter_context(nc.sbuf_tensor(name, shape, dt))

        def sem(name):
            return ctx.enter_context(nc.semaphore(name))

        whl = {n: [sb(f"w{n}_{part}", [P, DC, D], F16) for part in ("hi", "lo")] for n in "qkvo"}
        w1q = sb("w1_ternary", [P, DC, F], F8)
        w2q = sb("w2_ternary", [P, FC, D], F8)
        ctx_raw = sb("ctx_raw", [P, KT, D], F32)
        kh = sb("k_stage_hi", [P, DC, NK], F16)
        kl = sb("k_stage_lo", [P, DC, NK], F16)
        qk_full = sb("qk_full", [P, 2, 2 * NQ], F32)
        ctx_t = [sb(f"ctx_t_{part}", [P, DC, NK], F16) for part in ("hi", "lo")]
        x_t = [sb(f"x_t_{part}", [P, DC, NQ], F16) for part in ("hi", "lo")]
        qh = sb("q_stage_hi", [P, DC, NQ], F16)
        ql = sb("q_stage_lo", [P, DC, NQ], F16)
        v_stage = sb("v_stage", [P, KT, H, 2, VW], F16)
        v_flat = sb("v_now", [P, KT * H * 2 * VW], F16)
        v_now = v_flat[:, :].rearrange("p (i h s d) -> p i h s d", i=KT, h=H, s=2)
        k_flat = sb("k_stack", [P, H * NK], F16)
        k_stack = k_flat[:, :].rearrange("p (h n) -> p h n", h=H)
        q_stack = sb("q_stack", [P, H, NQ], F16)
        p_full = sb("p_full", [P, 2, 2 * NQ], F32)
        p_flat = sb("p_parts", [P, 2 * 6 * 2 * NQ], F16)
        p_parts = p_flat[:, :].rearrange("p (s u n) -> p s u n", s=2, u=6)
        ph, pl = p_parts[:, 0], p_parts[:, 1]
        h_flat = sb("h_parts", [P, 2 * FC * NQ], F16)
        h_parts = h_flat[:, :].rearrange("p (s c n) -> p s c n", s=2, c=FC)
        hh, hl = h_parts[:, 0], h_parts[:, 1]
        h_full = sb("h_full", [P, 2, 2 * NQ], F32)
        o_t = [sb(f"o_t_{part}", [P, DC, NQ], F16) for part in ("hi", "lo")]
        xq = sb("x_for_q", [P, 2, D], F32)
        xb = sb("x_residual", [P, 2, D], F32)
        o_sum = sb("o_sum", [P, 2, H, VW], F32)
        yo = sb("rows_to_turn", [P, 2, D], F32)
        bo_row = sb("bo_row", [P, D], F32)
        b2_row = sb("b2_row", [P, D], F32)
        ident = sb("ident", [P, P], F32)
        ident16 = sb("ident16", [P, P], F16)
        ones = sb("ones", [P, P], F32)
        col = sb("columns", [P, 44], F32)
        g2 = sb("gates", [P, 2], F32)
        gt = sb("gates_tanh", [P, 2], F32)
        gains = sb("gains", [P, 10], F32)
        bias = sb("bias", [P, 12], F32)
        bias4 = sb("bias4", [P, 8], F32)
        b1y = sb("b1_scaled", [P, FC], F32)
        bn1 = sb("bn1", [P, 8, 6], F32)
        mv1 = sb("mean_var1", [P, 8, 2], F32)
        r1 = sb("rstd1", [P, 5, 8], F32)
        bn2 = sb("bn2", [P, 2, 6], F32)
        mv2 = sb("mean_var2", [P, 2, 2], F32)
        r2 = sb("rstd2", [P, 5, 2], F32)
        minus_m = sb("minus_m", [48, H * NK // 48], F16)
        minus_half = sb("minus_half", [P, 8], F32)
        mx = sb("row_max", [P, H, 2], F32)
        mxs = sb("row_max_scaled", [P, 2, 2], F32)
        mhl = sb("row_max_parts", [P, H, 2, 2], F16)
        rden = sb("rden", [P, 2, H], F32)
        abs_sum = sb("abs_sum", [P, PIECES], F32)
        abs_tot = sb("abs_tot", [P, 2], F32)
        thr = sb("thresholds", [P, 4], F32)

        raw = {"k": k_flat[:, 0:2 * DC * D], "v": k_flat[:, 2 * DC * D:4 * DC * D],
               "q": v_flat[:, 0:2 * DC * D], "o": p_flat[:, 0:2 * DC * D]}
        raw = {n: a.bitcast(F32).rearrange("p (c n) -> p c n", c=DC) for n, a in raw.items()}
        piece = h_flat[:, 0:PIECE_RING * 2048].bitcast(F32).rearrange("p (r n) -> p r n", r=PIECE_RING)
        below = yo[:, :, :].rearrange("p a b -> p (a b)").bitcast(F16)[:, 0:1024]
        bv_wide = o_sum[:, :, :, :].rearrange("p a b c -> p (a b c)")[:, 0:DC * P]
        bv_wide = bv_wide.rearrange("p (c n) -> p c n", c=DC)

        ps_score = ctx.enter_context(nc.psum_tensor("ps_score", [P, 2, 512], F32))
        ps_exp = ctx.enter_context(nc.psum_tensor("ps_exp", [P, 2, 512], F32))
        ps_pv = ctx.enter_context(nc.psum_tensor("ps_pv", [P, 2, 512], F32))
        ps_fill = ctx.enter_context(nc.psum_tensor("ps_fill", [P, 2, 512], F32))

        ctx_loaded, x_loaded, xb_loaded = sem("ctx_loaded"), sem("x_loaded"), sem("xb_loaded")
        kq_landed = [sem(f"kq_landed{c}") for c in range(DC)]
        v_landed = [sem(f"v_landed{c}") for c in range(DC)]
        out_stored = sem("out_stored")
        w_loaded = {n: sem(f"w{n}_loaded") for n in "qkvo"}
        small_loaded = sem("small_loaded")
        piece_loaded = [sem(f"piece_loaded{r}") for r in range(PIECE_RING)]
        piece_summed, piece_done = sem("piece_summed"), sem("piece_done")
        piece_below = sem("piece_below")
        consts, passed, rows_set = sem("consts"), sem("passed"), sem("rows_set")
        gate_ready, gains_ready = sem("gate_ready"), sem("gains_ready")
        w_hi, w_split = sem("w_hi"), sem("w_split")
        bias_sums, bias_step, wide_ready = sem("bias_sums"), sem("bias_step"), sem("wide_ready")
        bo_sums, bo_step = sem("bo_sums"), sem("bo_step")
        tot_ready, tot_all, thr_step = sem("tot_ready"), sem("tot_all"), sem("thr_step")
        fill_ready = sem("fill_ready")
        scores_ready, max_taken = sem("scores_ready"), sem("max_taken")
        max_scaled, max_hi, max_split = sem("max_scaled"), sem("max_hi"), sem("max_split")
        shift_rows = sem("shift_rows")
        logits_ready, exp_done, p_split = sem("logits_ready"), sem("exp_done"), sem("p_split")
        pv_done, o_taken = sem("pv_done"), sem("o_taken")
        o_recip, o_normed = sem("o_recip"), sem("o_normed")
        stats1_step, stats1, rstd1_step = sem("stats1_step"), sem("stats1"), sem("rstd1_step")
        ctx_normed, x_normed = sem("ctx_normed"), sem("x_normed")
        stats2_step, stats2, rstd2_step = sem("stats2_step"), sem("stats2"), sem("rstd2_step")
        norm1_ready, norm2_ready = sem("norm1_ready"), sem("norm2_ready")
        y_normed = sem("y_normed")
        ctx_hi, ctx_split = sem("ctx_hi"), sem("ctx_split")
        x_hi, x_split = sem("x_hi"), sem("x_split")
        qk_lifted, qk_hi, qk_split = sem("qk_lifted"), sem("qk_hi"), sem("qk_split")
        v_hi, v_split = sem("v_hi"), sem("v_split")
        o_hi, o_split = sem("o_hi"), sem("o_split")
        xb_biased, x1_ready, x1_biased = sem("xb_biased"), sem("x1_ready"), sem("x1_biased")
        y_hi, y_split = sem("y_hi"), sem("y_split")
        h_lifted, h_hi, h_split = sem("h_lifted"), sem("h_hi"), sem("h_split")
        out_ready = sem("out_ready")

        FREED = {"cx": (ctx_split, 6, 0), "xx": (x_split, 2, 0), "q": (qk_lifted, 10, 0),
                 "k": (qk_lifted, 10, 2), "v": (v_split, 6, 0), "mr": (shift_rows, 8, 0),
                 "ot": (o_split, 2, 0), "op": (x1_ready, 2, 0), "yt": (y_split, 2, 0),
                 "f1": (h_lifted, 8, 0), "f2": (out_ready, 4, 4)}

        def batch_of(kind, i, b):
            return b + 1 if kind in PREP or i == -1 else b - 1 if kind in FINISH else b

        def freed(kind, i, b):
            s, per_batch, first = FREED[kind]
            return s, batch_of(kind, i, b) * per_batch + (first + max(i, 0) + 1)

        block = ctx.enter_context(nc.Block())

        def wait_alone(eng, s, value):
            eng.wait_ge(s, value)
            eng.sem_inc(passed, 1)

        def iterations(eng, body):
            body(-1, FIRST)
            body(0, SECOND)
            with eng.Fori(1, B - 1) as b:
                body(b, INNER)
            body(B - 1, LAST)
            body(B, TAIL)

        def q_cols(t):
            return slice(QNEW[t], P), slice(QSTART[t] + QNEW[t], QSTART[t] + P)

        @block.sync
        def _(sp):
            def load_ctx(n):
                sp.dma_start(ctx_raw[0:KR, :, :], ctx_in[n].rearrange("(i p) d -> p i d", p=KR)) \
                    .then_inc(ctx_loaded, 16)

            def load_x(n, dst, loaded):
                for t in range(2):
                    sp.dma_start(dst[:, t, :], x[n][QSTART[t]:QSTART[t] + P, :]).then_inc(loaded, 16)

            def copy_kq(g):
                for part, (ks, qs) in enumerate(((kh, qh), (kh, ql), (kl, qh))):
                    for stack, stage in ((q_stack, qs), (k_stack, ks)):
                        sp.dma_start(stack[HD * part:HD * part + HD, 4 * g:4 * g + 4, :],
                                     stage[HD * g:HD * g + HD, :, :]).then_inc(kq_landed[g], 16)

            def copy_v(c):
                sp.dma_start(v_now[0:KR, :, 4 * c:4 * c + 4], v_stage[0:KR, :, 4 * c:4 * c + 4]) \
                    .then_inc(v_landed[c], 16)

            def body(b, stages):
                attend, prep, finish = stages
                n = b + 1
                if prep and attend:
                    wait_alone(sp, ctx_split, n * 6)
                    load_ctx(n)
                    wait_alone(sp, x_split, n * 2)
                    load_x(n, xq, x_loaded)
                if attend:
                    if finish:
                        wait_alone(sp, pv_done, b * 16)
                    copy_v(3)
                if finish:
                    wait_alone(sp, out_stored, b * 32)
                    load_x(b - 1, xb, xb_loaded)
                if prep:
                    wait_alone(sp, qk_split, n * 10 + 10)
                    for c in range(DC):
                        if attend:
                            wait_alone(sp, logits_ready, b * 48 + 12 * (c + 1))
                        copy_kq(c)
                        if c == 1:
                            wait_alone(sp, v_split, n * 6 + 6)
                        if c >= 1:
                            if attend:
                                wait_alone(sp, pv_done, b * 16 + 4 * c)
                            copy_v(c - 1)
                if finish:
                    wait_alone(sp, out_ready, b * 4 + 4)
                    for t in range(2):
                        rows, to = q_cols(t)
                        sp.dma_start(out[b - 1][to, :], xb[rows, t, :]).then_inc(out_stored, 16)
            load_x(0, xq, x_loaded)
            load_ctx(0)
            sp.sem_inc(out_stored, 32)
            for a, b_ in ((col[:, :], cols), (g2[:, 0:1], g_x.partition_broadcast(P)),
                          (g2[:, 1:2], g_f.partition_broadcast(P)),
                          (bo_row[:, :], bo.partition_broadcast(P)), (b2_row[:, :], b2.partition_broadcast(P))):
                sp.dma_start(a, b_).then_inc(small_loaded, 16)
            for name, w in (("q", w_q), ("k", w_k), ("v", w_v), ("o", w_o)):
                sp.dma_start(raw[name], w.rearrange("(c p) n -> p c n", p=P)).then_inc(w_loaded[name], 16)
            sp.wait_ge(w_split, 4 * DC)
            sp.wait_ge(bias_sums, 3)
            sp.wait_ge(consts, 7)
            for row in range(SPLIT_ROWS, STACK_ROWS):
                sp.dma_start(k_flat[row:row + 1, :], minus_m[:, :]).then_inc(rows_set, 16)
            iterations(sp, body)
            sp.wait_ge(out_stored, B * 32 + 32)

        def load_piece(eng, k):
            k16 = k % PIECES
            if k16 < 8:
                src = w1t[(k16 // 2) * P:(k16 // 2 + 1) * P, (k16 % 2) * 1024:(k16 % 2 + 1) * 1024]
                dst = piece[:, k % PIECE_RING, :]
            else:
                src = w2t[(k16 - 8) * 2 * P:(k16 - 7) * 2 * P, :].rearrange("(c p) n -> p c n", p=P)
                dst = piece[:, k % PIECE_RING, :].rearrange("p (c n) -> p c n", c=2)
            eng.dma_start(dst, src).then_inc(piece_loaded[k % PIECE_RING], 16)

        @block.tensor
        def _(pe):
            def three(out_ap, left, right, order=((0, 0), (0, 1), (1, 0)), chunks=DC):
                n = 0
                for c in range(chunks):
                    for a, b_ in order:
                        last = pe.matmul(out_ap, left(a, c), right(b_, c), start=(n == 0),
                                         stop=(n == chunks * len(order) - 1))
                        n += 1
                return last

            def score(n, h, t):
                if t == 0 and h % 4 == 0:
                    pe.wait_ge(kq_landed[h // 4], n * 96 + 96)
                if not (isinstance(n, int) and n == 0 and h + t == 0):
                    pe.wait_ge(max_taken, n * 32 + (2 * h + t))
                for half in range(2):
                    last = pe.matmul(ps_score[:, half, 0:KH],
                                     q_stack[0:SPLIT_ROWS, h, QSTART[t]:QSTART[t] + P],
                                     k_stack[0:SPLIT_ROWS, h, half * KH:half * KH + KH],
                                     start=True, stop=True)
                last.then_inc(scores_ready, 1)

            def expo(b, h, u):
                if u == 0 and h % 2 == 0:
                    pe.wait_ge(shift_rows, b * 8 + (h // 2 + 1))
                if not (isinstance(b, int) and b * 48 + 3 * h + u < 2):
                    pe.wait_ge(exp_done, b * 48 + (3 * h + u - 1))
                for kt in (2 * u, 2 * u + 1):
                    last = pe.matmul(ps_exp[0:KR, (3 * h + u) % 2, (kt % 2) * NQ:(kt % 2) * NQ + NQ],
                                     k_stack[0:STACK_ROWS, h, kt * KR:kt * KR + KR],
                                     q_stack[0:STACK_ROWS, h, :], start=True, stop=True)
                last.then_inc(logits_ready, 1)

            def pv(b, h):
                if h % 4 == 0:
                    pe.wait_ge(v_landed[h // 4], b * 16 + 16)
                pe.wait_ge(p_split, b * 48 + (3 * h + 3))
                if not (isinstance(b, int) and b * 16 + h < 2):
                    pe.wait_ge(o_taken, b * 16 + (h - 1))
                for t in range(2):
                    for kt in range(KT):
                        for part in (ph, pl):
                            q0 = (kt % 2) * NQ + QSTART[t]
                            last = pe.matmul(
                                ps_pv[:, h % 2, t * 2 * VW:(t + 1) * 2 * VW],
                                part[0:KR, 3 * (h % 2) + kt // 2, q0:q0 + P],
                                v_now[0:KR, kt, h].rearrange("p a b -> p (a b)"),
                                start=(kt == 0 and part is ph), stop=(kt == KT - 1 and part is pl))
                last.then_inc(pv_done, 1)

            def turn(rows, bank, src, size=P):
                for c in range(DC):
                    last = pe.transpose(ps_fill[:, bank, c * size:(c + 1) * size],
                                        src[0:rows, c * P:(c + 1) * P], ident[0:rows, 0:rows])
                return last

            def fill(kind, i, b, bank):
                n, p_ = b + 1, b - 1
                if kind == "cx":
                    pe.wait_ge(ctx_normed, n * 6 + (i + 1))
                    last = turn(KR, bank, ctx_raw[:, i, :], KR)
                elif kind == "xx":
                    pe.wait_ge(x_normed, n * 2 + (i + 1))
                    last = turn(P, bank, xq[:, i, :])
                elif kind == "q":
                    if i == 0:
                        pe.wait_ge(x_split, n * 2 + 2)
                        if isinstance(b, int) and b == -1:
                            pe.wait_ge(w_split, DC)
                    for j in range(2):
                        m = slice((2 * i + j) * P, (2 * i + j + 1) * P)
                        last = three(ps_fill[:, bank, j * NQ:(j + 1) * NQ],
                                     lambda a, c: whl["q"][a][:, c, m], lambda a, c: x_t[a][:, c, :])
                elif kind == "k":
                    if i == 0:
                        pe.wait_ge(ctx_split, n * 6 + 6)
                        if isinstance(b, int) and b == -1:
                            pe.wait_ge(w_split, 2 * DC)
                    m, r = slice((i // 2) * P, (i // 2 + 1) * P), slice((i % 2) * KH, (i % 2 + 1) * KH)
                    last = three(ps_fill[:, bank, 0:KH], lambda a, c: whl["k"][a][:, c, m],
                                 lambda a, c: ctx_t[a][:, c, r])
                elif kind == "v":
                    if i == 0 and isinstance(b, int) and b == -1:
                        pe.wait_ge(w_split, 3 * DC)
                    r = slice(i * KR, (i + 1) * KR)
                    last = three(ps_fill[0:KR, bank, :], lambda a, c: ctx_t[a][:, c, r],
                                 lambda a, c: whl["v"][a][:, c, :])
                elif kind == "mr":
                    m, nb = (i, b) if i > 0 else (0, n)
                    pe.wait_ge(max_split, nb * 8 + (m + 1))
                    for h in (2 * m, 2 * m + 1):
                        for t in range(2):
                            frm, to = q_cols(t)
                            last = pe.matmul(
                                ps_fill[SPLIT_ROWS:STACK_ROWS, bank, (h % 2) * NQ + to.start:(h % 2) * NQ + to.stop],
                                mhl[:, h, t, :], ident16[:, frm], start=True, stop=True,
                                tile_position=(0, SPLIT_ROWS))
                elif kind == "ot":
                    pe.wait_ge(o_normed, p_ * 2 + (i + 1))
                    last = turn(P, bank, yo[:, i, :])
                elif kind == "op":
                    if i == 0:
                        pe.wait_ge(o_split, p_ * 2 + 2)
                    last = three(ps_fill[:, bank, :], lambda a, c: o_t[a][:, c, QSTART[i]:QSTART[i] + P],
                                 lambda a, c: whl["o"][a][:, c, :])
                elif kind == "yt":
                    pe.wait_ge(y_normed, p_ * 2 + (i + 1))
                    last = turn(P, bank, yo[:, i, :])
                elif kind == "f1":
                    if i == 0:
                        wait_alone(pe, y_split, p_ * 2 + 2)
                        if not isinstance(b, int):
                            pe.wait_ge(piece_done, PIECES)
                    for j in range(2):
                        m = slice((2 * i + j) * P, (2 * i + j + 1) * P)
                        last = three(ps_fill[:, bank, j * NQ:(j + 1) * NQ], lambda a, c: w1q[:, c, m],
                                     lambda a, c: o_t[a][:, c, :], order=((0, 0), (0, 1)))
                else:
                    if i == 0:
                        wait_alone(pe, h_split, p_ * 8 + 8)
                    t, w = i // 2, slice((i % 2) * 256, (i % 2 + 1) * 256)
                    r = slice(QSTART[t], QSTART[t] + P)
                    last = three(ps_fill[:, bank, 0:256], lambda a, c: (hh, hl)[a][:, c, r],
                                 lambda a, c: w2q[:, c, w], order=((0, 0), (1, 0)), chunks=FC)
                last.then_inc(fill_ready, 1)

            def before(stages):
                return {SECOND: FIRST, INNER: SECOND, LAST: INNER, TAIL: LAST}[stages]

            def body(b, stages):
                done = []
                if stages != FIRST:
                    for kind, i in fill_list(before(stages))[-2:]:
                        pe.wait_ge(*freed(kind, i, b - 1))
                    if stages == INNER:
                        for kind, i in fill_list(INNER)[-2:]:
                            pe.wait_ge(*freed(kind, i, b - 1))
                for slot in range(H):
                    for kind, i in slot_steps(slot, *stages):
                        if kind == "score":
                            h = (slot + 4) % H
                            score(b + 1 if slot >= 12 else b, h, i)
                        elif kind == "expo":
                            expo(b, slot, i)
                        elif kind == "pv":
                            pv(b if slot else b - 1, i)
                        else:
                            if len(done) >= 2:
                                if kind in ("f1", "f2"):
                                    wait_alone(pe, *freed(*done[-2], b))
                                else:
                                    pe.wait_ge(*freed(*done[-2], b))
                            fill(kind, i, b, len(done) % 2)
                            done.append((kind, i))

            pe.wait_ge(consts, 5)
            pe.wait_ge(small_loaded, 80)
            for at, (name, beta) in enumerate((("q", 16), ("k", 24), ("v", 24))):
                pe.wait_ge(w_loaded[name], 16)
                for m in range(DC):
                    for c in range(DC):
                        last = pe.matmul(ps_pv[:, 0, at * DC + m:at * DC + m + 1],
                                         raw[name][:, c, m * P:(m + 1) * P], col[:, beta + c:beta + c + 1],
                                         start=(c == 0), stop=(c == DC - 1))
                last.then_inc(bias_sums, 1)
            pe.wait_ge(wide_ready, DC)
            pe.wait_ge(w_loaded["o"], 16)
            for c in range(DC):
                last = pe.matmul(ps_pv[:, 1, :], bv_wide[:, c, :], raw["o"][:, c, :],
                                 start=(c == 0), stop=(c == DC - 1))
            last.then_inc(bo_sums, 1)
            body(-1, FIRST)
            pe.wait_ge(tot_ready, 2)
            pe.matmul(ps_pv[:, 0, 0:2], ones[:, :], abs_tot[:, :], start=True, stop=True).then_inc(tot_all, 1)
            pe.wait_ge(thr_step, 1)
            pe.wait_ge(rows_set, 32)
            body(0, SECOND)
            with pe.Fori(1, B - 1) as b:
                body(b, INNER)
            body(B - 1, LAST)
            body(B, TAIL)

        @block.scalar
        def _(act):
            def expo(b, h, u):
                k = 3 * h + u
                act.wait_ge(logits_ready, b * 48 + (k + 1))
                if not (isinstance(b, int) and b * 48 + k < 2):
                    act.wait_ge(p_split, b * 48 + (k - 1))
                if u == 0 and not (isinstance(b, int) and b * 16 + h < 2):
                    act.wait_ge(pv_done, b * 16 + (h - 1))
                unit = 3 * (h % 2) + u
                nc.scalar.activation(p_full[0:KR, k % 2, :], ps_exp[0:KR, k % 2, 0:2 * NQ], ACT.Exp,
                                     scale=EXP_SCALE)
                nc.scalar.activation(ph[0:KR, unit, :], ps_exp[0:KR, k % 2, 0:2 * NQ], ACT.Exp,
                                     scale=EXP_SCALE).then_inc(exp_done, 1)

            def fill(kind, i, b, bank, ready):
                n, p_ = b + 1, b - 1
                if kind in ("op", "f2"):
                    return
                act.wait_ge(fill_ready, ready)
                if kind == "cx":
                    nc.scalar.activation(ctx_t[0][:, :, i * KR:(i + 1) * KR],
                                         ps_fill[:, bank, 0:DC * KR].rearrange("p (c n) -> p c n", c=DC),
                                         ACT.Copy, scale=Z_SCALE).then_inc(ctx_hi, 1)
                elif kind in ("xx", "ot", "yt"):
                    dst, scale, s = {"xx": (x_t, Z_SCALE, x_hi), "ot": (o_t, 1.0, o_hi),
                                     "yt": (o_t, Y_SCALE, y_hi)}[kind]
                    frm, to = q_cols(i)
                    src = ps_fill[:, bank, :].rearrange("p (c n) -> p c n", c=DC)[:, :, frm]
                    nc.scalar.activation(dst[0][:, :, to], src, ACT.Copy, scale=scale).then_inc(s, 1)
                elif kind == "q":
                    if isinstance(b, int) and b == -1 and i == 0:
                        act.wait_ge(bias_step, 3)
                    if not (isinstance(b, int) and b == -1):
                        act.wait_ge(qk_split, n * 10 + (i - 1))
                    for j in range(2):
                        last = nc.scalar.activation(qk_full[:, i % 2, j * NQ:(j + 1) * NQ],
                                                    ps_fill[:, bank, j * NQ:(j + 1) * NQ], ACT.Identity,
                                                    bias=bias4[:, 2 * i + j:2 * i + j + 1], scale=PSUM_TO_QK)
                    last.then_inc(qk_lifted, 1)
                elif kind == "k":
                    act.wait_ge(qk_split, n * 10 + (i + 1))
                    nc.scalar.activation(qk_full[:, i % 2, 0:KH], ps_fill[:, bank, 0:KH], ACT.Identity,
                                         bias=bias4[:, 4 + i // 2:5 + i // 2],
                                         scale=PSUM_TO_QK).then_inc(qk_lifted, 1)
                elif kind == "v":
                    if i == 0 and not (isinstance(b, int) and b == -1):
                        act.wait_ge(v_landed[3], n * 16)
                    nc.scalar.activation(v_stage[0:KR, i, :, 0, 0:HD],
                                         ps_fill[0:KR, bank, :].rearrange("p (h d) -> p h d", h=H),
                                         ACT.Copy, scale=PSUM_TO_V).then_inc(v_hi, 1)
                elif kind == "mr":
                    m = max(i, 0)
                    nc.scalar.activation(q_stack[SPLIT_ROWS:STACK_ROWS, 2 * m:2 * m + 2, :],
                                         ps_fill[SPLIT_ROWS:STACK_ROWS, bank, 0:2 * NQ]
                                         .rearrange("p (h n) -> p h n", h=2), ACT.Copy).then_inc(shift_rows, 1)
                elif kind == "f1":
                    if i >= 2:
                        act.wait_ge(h_split, p_ * 8 + (i - 1))
                    for j in range(2):
                        last = nc.scalar.activation(h_full[:, i % 2, j * NQ:(j + 1) * NQ],
                                                    ps_fill[:, bank, j * NQ:(j + 1) * NQ], ACT.Relu,
                                                    bias=b1y[:, 2 * i + j:2 * i + j + 1])
                    last.then_inc(h_lifted, 1)

            def norm_prep(n):
                act.wait_ge(norm1_ready, n + 1)
                for t in range(2):
                    j = KT + t
                    nc.scalar.activation(xq[:, t, :], xq[:, t, :], ACT.Identity, bias=r1[:, 4, j:j + 1],
                                         scale=r1[:, 3, j:j + 1]).then_inc(x_normed, 1)
                for i in range(KT):
                    nc.scalar.activation(ctx_raw[0:KR, i, :], ctx_raw[0:KR, i, :], ACT.Identity,
                                         bias=r1[0:KR, 4, i:i + 1], scale=r1[0:KR, 3, i:i + 1]) \
                        .then_inc(ctx_normed, 1)

            def norm_finish(p_):
                act.wait_ge(norm2_ready, p_ + 1)
                act.wait_ge(o_split, p_ * 2 + 2)
                for t in range(2):
                    nc.scalar.activation(yo[:, t, :], xb[:, t, :], ACT.Identity, bias=r2[:, 4, t:t + 1],
                                         scale=r2[:, 3, t:t + 1]).then_inc(y_normed, 1)

            def sum_piece(k):
                act.wait_ge(piece_loaded[k % PIECE_RING], 16 * (k // PIECE_RING + 1))
                nc.scalar.activation(piece[:, k % PIECE_RING, :], piece[:, k % PIECE_RING, :], ACT.Abs,
                                     accum_out=abs_sum[:, k:k + 1]).then_inc(piece_summed, 1)
                act.wait_ge(piece_summed, k + 1)
                load_piece(act, k + PIECE_RING)

            def body(b, stages):
                done = 0
                attend, prep, finish = stages
                for slot in range(H):
                    if stages == FIRST:
                        sum_piece(slot)
                    if slot == 4 and finish:
                        norm_finish(b - 1)
                    if slot == (4 if attend else 3) and prep:
                        norm_prep(b + 1)
                    if stages == SECOND and slot >= 1 and PIECES + slot + 2 < 2 * PIECES:
                        act.wait_ge(piece_done, slot)
                        load_piece(act, PIECES + slot + 2)
                    for kind, i in slot_steps(slot, *stages):
                        if kind == "expo":
                            expo(b, slot, i)
                        elif kind in FILL_KINDS:
                            fill(kind, i, b, done % 2, fills_before(b) + (done + 1))
                            done += 1

            for k in range(PIECE_RING):
                load_piece(act, k)
            act.wait_ge(small_loaded, 80)
            nc.scalar.activation(gt[:, :], g2[:, :], ACT.Tanh).then_inc(gate_ready, 1)
            act.wait_ge(gains_ready, 4)
            for name, at in (("q", 0), ("k", 4), ("v", 4), ("o", None)):
                act.wait_ge(w_loaded[name], 16)
                for c in range(DC):
                    gain = gains[:, 8:9] if at is None else gains[:, at + c:at + c + 1]
                    nc.scalar.activation(whl[name][0][:, c, :], raw[name][:, c, :], ACT.Copy,
                                         scale=gain).then_inc(w_hi, 1)
            body(-1, FIRST)
            act.wait_ge(w_split, 4 * DC)
            act.wait_ge(bo_sums, 1)
            body(0, SECOND)
            with act.Fori(1, B - 1) as b:
                body(b, INNER)
            body(B - 1, LAST)
            body(B, TAIL)

        @block.vector
        def _(dve):
            def score(n, h, t):
                dve.wait_ge(scores_ready, n * 32 + (2 * h + t + 1))
                nc.vector.tensor_reduce(mx[:, h, t:t + 1], ps_score[:, :, 0:KH], AX.XY, ALU.max) \
                    .then_inc(max_taken, 1)

            def split_max(n, m):
                dve.wait_ge(max_taken, n * 32 + (4 * m + 4))
                nc.vector.tensor_scalar(mxs[:, :, :], mx[:, 2 * m:2 * m + 2, :], 1.0 / M_SCALE, -MAX_SHIFT,
                                        ALU.mult, ALU.add).then_inc(max_scaled, 1)
                dve.wait_ge(max_scaled, n * 8 + (m + 1))
                nc.vector.tensor_copy(mhl[:, 2 * m:2 * m + 2, :, 0], mxs[:, :, :]).then_inc(max_hi, 1)
                dve.wait_ge(max_hi, n * 8 + (m + 1))
                nc.vector.tensor_tensor(mhl[:, 2 * m:2 * m + 2, :, 1], mxs[:, :, :],
                                        mhl[:, 2 * m:2 * m + 2, :, 0], ALU.subtract).then_inc(max_split, 1)

            def expo(b, h, u):
                k, unit = 3 * h + u, 3 * (h % 2) + u
                dve.wait_ge(exp_done, b * 48 + (k + 1))
                nc.vector.tensor_tensor(pl[0:KR, unit, :], p_full[0:KR, k % 2, :], ph[0:KR, unit, :],
                                        ALU.subtract).then_inc(p_split, 1)

            def take_o(b, h):
                dve.wait_ge(pv_done, b * 16 + (h + 1))
                if h == 0 and not (isinstance(b, int) and b == 0):
                    dve.wait_ge(o_normed, b * 2)
                nc.vector.tensor_reduce(o_sum[:, :, h, :],
                                        ps_pv[:, h % 2, 0:4 * VW].rearrange("p (t s d) -> p t d s", t=2, s=2),
                                        AX.X, ALU.add).then_inc(o_taken, 1)

            def normalise(b):
                dve.wait_ge(o_taken, b * 16 + 16)
                nc.vector.reciprocal(rden[:, :, :], o_sum[:, :, :, HD]).then_inc(o_recip, 1)
                dve.wait_ge(o_recip, b + 1)
                for t in range(2):
                    nc.vector.tensor_tensor(yo[:, t, :].rearrange("p (h d) -> p h d", h=H),
                                            o_sum[:, t, :, 0:HD],
                                            rden[:, t, :].unsqueeze(2).to_broadcast([P, H, HD]),
                                            ALU.mult).then_inc(o_normed, 1)

            def stats_prep(n):
                dve.wait_ge(ctx_loaded, n * 16 + 16)
                dve.wait_ge(x_loaded, n * 32 + 32)
                if not (isinstance(n, int) and n == 0):
                    dve.wait_ge(ctx_normed, n * 6)
                for i in range(KT):
                    nc.vector.bn_stats(bn1[0:KR, i, :], ctx_raw[0:KR, i, :])
                for t in range(2):
                    last = nc.vector.bn_stats(bn1[:, KT + t, :], xq[:, t, :])
                last.then_inc(stats1_step, 1)
                wait_alone(dve, stats1_step, n + 1)
                for i in range(KT):
                    nc.vector.bn_aggr(mv1[0:KR, i, :], bn1[0:KR, i, :])
                for t in range(2):
                    last = nc.vector.bn_aggr(mv1[:, KT + t, :], bn1[:, KT + t, :])
                last.then_inc(stats1, 1)

            def stats_finish(p_):
                for t in range(2):
                    dve.wait_ge(x1_ready, p_ * 2 + (t + 1))
                    last = nc.vector.bn_stats(bn2[:, t, :], xb[:, t, :])
                last.then_inc(stats2_step, 1)
                wait_alone(dve, stats2_step, p_ + 1)
                for t in range(2):
                    last = nc.vector.bn_aggr(mv2[:, t, :], bn2[:, t, :])
                last.then_inc(stats2, 1)

            def fill(kind, i, b, bank, ready):
                n, p_ = b + 1, b - 1
                if kind == "cx":
                    dve.wait_ge(ctx_hi, n * 6 + (i + 1))
                    r = slice(i * KR, (i + 1) * KR)
                    nc.vector.scalar_tensor_tensor(
                        ctx_t[1][:, :, r], ps_fill[:, bank, 0:DC * KR].rearrange("p (c n) -> p c n", c=DC),
                        Z_SCALE, ctx_t[0][:, :, r], ALU.mult, ALU.subtract).then_inc(ctx_split, 1)
                elif kind in ("xx", "ot", "yt"):
                    dst, scale, hi, s = {"xx": (x_t, Z_SCALE, x_hi, x_split), "ot": (o_t, 1.0, o_hi, o_split),
                                         "yt": (o_t, Y_SCALE, y_hi, y_split)}[kind]
                    dve.wait_ge(hi, (n if kind == "xx" else p_) * 2 + (i + 1))
                    frm, to = q_cols(i)
                    src = ps_fill[:, bank, :].rearrange("p (c n) -> p c n", c=DC)[:, :, frm]
                    nc.vector.scalar_tensor_tensor(dst[1][:, :, to], src, scale, dst[0][:, :, to],
                                                   ALU.mult, ALU.subtract).then_inc(s, 1)
                elif kind == "q":
                    if i == 0 and not (isinstance(b, int) and b == -1):
                        for g in range(4):
                            dve.wait_ge(kq_landed[g], n * 96)
                    dve.wait_ge(qk_lifted, n * 10 + (i + 1))
                    nc.vector.tensor_copy(qh[:, 2 * i:2 * i + 2, :],
                                          qk_full[:, i % 2, 0:2 * NQ].rearrange("p (c n) -> p c n", c=2)) \
                        .then_inc(qk_hi, 1)
                elif kind == "k":
                    dve.wait_ge(qk_lifted, n * 10 + (i + 3))
                    nc.vector.tensor_copy(kh[:, i // 2, (i % 2) * KH:(i % 2 + 1) * KH],
                                          qk_full[:, i % 2, 0:KH]).then_inc(qk_hi, 1)
                elif kind == "v":
                    dve.wait_ge(v_hi, n * 6 + (i + 1))
                    nc.vector.scalar_tensor_tensor(
                        v_stage[0:KR, i, :, 1, 0:HD], ps_fill[0:KR, bank, :].rearrange("p (h d) -> p h d", h=H),
                        PSUM_TO_V, v_stage[0:KR, i, :, 0, 0:HD], ALU.mult, ALU.subtract).then_inc(v_split, 1)
                elif kind == "op":
                    dve.wait_ge(fill_ready, ready)
                    dve.wait_ge(xb_biased, p_ * 2 + (i + 1))
                    nc.vector.scalar_tensor_tensor(xb[:, i, :], ps_fill[:, bank, :], PSUM_TO_O, xb[:, i, :],
                                                   ALU.mult, ALU.add).then_inc(x1_ready, 1)
                    if i == 1:
                        stats_finish(p_)
                elif kind == "f1":
                    dve.wait_ge(h_lifted, p_ * 8 + (i + 1))
                    nc.vector.tensor_copy(hh[:, 2 * i:2 * i + 2, :],
                                          h_full[:, i % 2, :].rearrange("p (c n) -> p c n", c=2)) \
                        .then_inc(h_hi, 1)
                elif kind == "f2":
                    dve.wait_ge(fill_ready, ready)
                    dve.wait_ge(x1_biased, p_ * 2 + (i // 2 + 1))
                    w = slice((i % 2) * 256, (i % 2 + 1) * 256)
                    nc.vector.scalar_tensor_tensor(xb[:, i // 2, w], ps_fill[:, bank, 0:256], gains[:, 9:10],
                                                   xb[:, i // 2, w], ALU.mult, ALU.add).then_inc(out_ready, 1)

            def quantise(k):
                j = k // 8
                kk = PIECES + k
                src = piece[:, kk % PIECE_RING, :]
                dst = w1q[:, k // 2, (k % 2) * 1024:(k % 2 + 1) * 1024] if k < 8 else \
                    w2q[:, 2 * (k - 8):2 * (k - 8) + 2, :].rearrange("p c n -> p (c n)")
                dve.wait_ge(piece_loaded[kk % PIECE_RING], 16 * (kk // PIECE_RING + 1))
                if k:
                    dve.wait_ge(piece_done, k)
                nc.vector.tensor_scalar(below, src, thr[:, 2 + j:3 + j], None, ALU.is_lt).then_inc(piece_below, 1)
                dve.wait_ge(piece_below, k + 1)
                nc.vector.scalar_tensor_tensor(dst, src, thr[:, j:j + 1], below, ALU.is_gt, ALU.subtract,
                                               saturate=False) \
                    .then_inc(piece_done, 1)

            def body(b, stages):
                done = 0
                attend, prep, finish = stages
                for slot in range(H):
                    if slot == 2 and prep and attend:
                        stats_prep(b + 1)
                    if stages == SECOND:
                        quantise(slot)
                    if slot == 1 and finish:
                        normalise(b - 1)
                    m = slot // 2 + 1
                    if slot % 2 == 0 and (prep if m == H // 2 else attend):
                        split_max(b if m < H // 2 else b + 1, m % (H // 2))
                    for kind, i in slot_steps(slot, *stages):
                        if kind == "score":
                            score(b + 1 if slot >= 12 else b, (slot + 4) % H, i)
                        elif kind == "expo":
                            expo(b, slot, i)
                        elif kind == "pv":
                            take_o(b if slot else b - 1, i)
                        else:
                            fill(kind, i, b, done % 2, fills_before(b) + (done + 1))
                            done += 1

            dve.wait_ge(consts, 5)
            nc.vector.memset(thr[:, :], 0.0).then_inc(out_ready, 4)
            stats_prep(0)
            dve.wait_ge(small_loaded, 80)
            nc.vector.tensor_scalar(gains[:, 0:4], col[:, 12:16], W_SCALE, None, ALU.mult).then_inc(gains_ready, 1)
            nc.vector.tensor_scalar(gains[:, 4:8], col[:, 20:24], W_SCALE, None, ALU.mult).then_inc(gains_ready, 1)
            dve.wait_ge(gate_ready, 1)
            nc.vector.tensor_scalar(gains[:, 8:9], gt[:, 0:1], W_SCALE, None, ALU.mult).then_inc(gains_ready, 1)
            nc.vector.tensor_scalar(gains[:, 9:10], gt[:, 1:2], 1.0 / Y_SCALE, None, ALU.mult) \
                .then_inc(gains_ready, 1)
            nc.vector.tensor_scalar(b1y[:, :], col[:, 28:44], Y_SCALE, None, ALU.mult)
            nc.vector.tensor_scalar(b2_row[:, :], b2_row[:, :], gt[:, 1:2], None, ALU.mult).then_inc(bo_step, 1)
            dve.wait_ge(gains_ready, 4)
            for w, (name, at) in enumerate((("q", 0), ("k", 4), ("v", 4), ("o", None))):
                for c in range(DC):
                    dve.wait_ge(w_hi, w * DC + c + 1)
                    gain = gains[:, 8:9] if at is None else gains[:, at + c:at + c + 1]
                    nc.vector.scalar_tensor_tensor(whl[name][1][:, c, :], raw[name][:, c, :], gain,
                                                   whl[name][0][:, c, :], ALU.mult, ALU.subtract) \
                        .then_inc(w_split, 1)
                if name == "v":
                    dve.wait_ge(bias_sums, 3)
                    nc.vector.tensor_tensor(bias[:, :], ps_pv[:, 0, 0:12], col[:, 0:12], ALU.add) \
                        .then_inc(bias_step, 1)
                    dve.wait_ge(bias_step, 1)
                    nc.vector.tensor_scalar(bias4[:, :], bias[:, 0:8], QK_SCALE, None, ALU.mult) \
                        .then_inc(bias_step, 2)
                    dve.wait_ge(consts, 5)
                    for c in range(DC):
                        nc.vector.tensor_scalar(bv_wide[:, c, :], ones[:, :], bias[:, 8 + c:9 + c], None,
                                                ALU.mult).then_inc(wide_ready, 1)
            dve.wait_ge(bo_sums, 1)
            nc.vector.tensor_tensor(bo_row[:, :], ps_pv[:, 1, :], bo_row[:, :], ALU.add).then_inc(bo_step, 1)
            dve.wait_ge(bo_step, 2)
            nc.vector.tensor_scalar(bo_row[:, :], bo_row[:, :], gt[:, 0:1], None, ALU.mult).then_inc(bo_step, 1)
            body(-1, FIRST)
            dve.wait_ge(piece_summed, PIECES)
            for j in range(2):
                nc.vector.tensor_reduce(abs_tot[:, j:j + 1], abs_sum[:, 8 * j:8 * j + 8], AX.X, ALU.add) \
                    .then_inc(tot_ready, 1)
            dve.wait_ge(tot_all, 1)
            nc.vector.tensor_scalar(thr[:, 0:2], ps_pv[:, 0, 0:2], 0.5 / (D * F), 0.5 * EPS, ALU.mult, ALU.add) \
                .then_inc(thr_step, 1)
            dve.wait_ge(thr_step, 1)
            nc.vector.tensor_scalar(thr[:, 2:4], thr[:, 0:2], -1.0, None, ALU.mult).then_inc(thr_step, 1)
            dve.wait_ge(thr_step, 2)
            body(0, SECOND)
            with dve.Fori(1, B - 1) as b:
                body(b, INNER)
            body(B - 1, LAST)
            body(B, TAIL)

        @block.gpsimd
        def _(pool):
            def rstd(r, step, base, width, mean, done):
                nc.gpsimd.tensor_tensor(r[:, 1, :], r[:, 0, :], minus_half[:, 0:width], ALU.pow).then_inc(step, 1)
                pool.wait_ge(step, base + 1)
                nc.gpsimd.tensor_tensor(r[:, 2, :], r[:, 1, :], r[:, 1, :], ALU.mult).then_inc(step, 1)
                pool.wait_ge(step, base + 2)
                nc.gpsimd.tensor_tensor(r[:, 2, :], r[:, 2, :], r[:, 0, :], ALU.mult).then_inc(step, 1)
                wait_alone(pool, step, base + 3)
                nc.gpsimd.tensor_scalar(r[:, 2, :], r[:, 2, :], -0.5, 1.5, ALU.mult, ALU.add).then_inc(step, 1)
                pool.wait_ge(step, base + 4)
                nc.gpsimd.tensor_tensor(r[:, 3, :], r[:, 1, :], r[:, 2, :], ALU.mult).then_inc(step, 1)
                pool.wait_ge(step, base + 5)
                nc.gpsimd.tensor_tensor(r[:, 4, :], mean, r[:, 3, :], ALU.mult).then_inc(step, 1)
                wait_alone(pool, step, base + 6)
                nc.gpsimd.tensor_scalar(r[:, 4, :], r[:, 4, :], -1.0, None, ALU.mult).then_inc(done, 1)

            def norm_prep(n):
                wait_alone(pool, stats1, n + 1)
                nc.gpsimd.tensor_scalar(r1[:, 0, 0:KT], mv1[:, 0:KT, 1], EPS, None, ALU.add).then_inc(rstd1_step, 1)
                nc.gpsimd.tensor_scalar(r1[:, 0, KT:8], mv1[:, KT:8, 1], 1.0 + EPS, EPS * EPS, ALU.mult, ALU.add) \
                    .then_inc(rstd1_step, 1)
                pool.wait_ge(rstd1_step, n * 8 + 2)
                rstd(r1, rstd1_step, n * 8 + 2, 8, mv1[:, :, 0], norm1_ready)

            def norm_finish(p_):
                wait_alone(pool, stats2, p_ + 1)
                nc.gpsimd.tensor_scalar(r2[:, 0, :], mv2[:, :, 1], EPS, None, ALU.add).then_inc(rstd2_step, 1)
                pool.wait_ge(rstd2_step, p_ * 7 + 1)
                rstd(r2, rstd2_step, p_ * 7 + 1, 2, mv2[:, :, 0], norm2_ready)
                pool.wait_ge(y_normed, p_ * 2 + 2)
                for t in range(2):
                    nc.gpsimd.tensor_tensor(xb[:, t, :], xb[:, t, :], b2_row[:, :], ALU.add).then_inc(x1_biased, 1)

            def bias_residual(p_):
                pool.wait_ge(xb_loaded, p_ * 32 + 32)
                for t in range(2):
                    nc.gpsimd.tensor_tensor(xb[:, t, :], xb[:, t, :], bo_row[:, :], ALU.add).then_inc(xb_biased, 1)

            def fill(kind, i, b):
                n, p_ = b + 1, b - 1
                if kind == "q":
                    pool.wait_ge(qk_hi, n * 10 + (i + 1))
                    nc.gpsimd.tensor_tensor(ql[:, 2 * i:2 * i + 2, :],
                                            qk_full[:, i % 2, 0:2 * NQ].rearrange("p (c n) -> p c n", c=2),
                                            qh[:, 2 * i:2 * i + 2, :], ALU.subtract).then_inc(qk_split, 1)
                elif kind == "k":
                    pool.wait_ge(qk_hi, n * 10 + (i + 3))
                    r = slice((i % 2) * KH, (i % 2 + 1) * KH)
                    nc.gpsimd.tensor_tensor(kl[:, i // 2, r], qk_full[:, i % 2, 0:KH], kh[:, i // 2, r],
                                            ALU.subtract).then_inc(qk_split, 1)
                elif kind == "f1":
                    pool.wait_ge(h_hi, p_ * 8 + (i + 1))
                    nc.gpsimd.tensor_tensor(hl[:, 2 * i:2 * i + 2, :],
                                            h_full[:, i % 2, :].rearrange("p (c n) -> p c n", c=2),
                                            hh[:, 2 * i:2 * i + 2, :], ALU.subtract).then_inc(h_split, 1)

            def body(b, stages):
                attend, prep, finish = stages
                for slot in range(H):
                    if slot == 1 and finish:
                        bias_residual(b - 1)
                    if slot == 2 and prep:
                        norm_prep(b + 1)
                    if slot == 3 and finish:
                        norm_finish(b - 1)
                    for kind, i in slot_steps(slot, *stages):
                        fill(kind, i, b)

            nc.gpsimd.memset(ident[:, :], 0.0).then_inc(consts, 1)
            pool.wait_ge(consts, 1)
            nc.gpsimd.affine_select(out=ident[:, :], in_=ident[:, :], compare_op=ALU.not_equal, fill=1.0,
                                    base=0, pattern=[[-1, P]], channel_multiplier=1).then_inc(consts, 1)
            pool.wait_ge(consts, 2)
            nc.gpsimd.tensor_copy(ident16[:, :], ident[:, :]).then_inc(consts, 1)
            nc.gpsimd.memset(ones[:, :], 1.0).then_inc(consts, 1)
            nc.gpsimd.memset(minus_half[:, :], -0.5)
            nc.gpsimd.memset(mv1[:, :, :], 1.0)
            nc.gpsimd.memset(v_stage[:, :, :, :, HD:VW], 0.0).then_inc(consts, 1)
            pool.wait_ge(consts, 5)
            nc.gpsimd.memset(v_stage[:, :, :, 0, HD:VW], 1.0).then_inc(consts, 1)
            nc.gpsimd.memset(minus_m[:, :], -M_SCALE).then_inc(consts, 1)
            pool.wait_ge(bo_step, 3)
            iterations(pool, body)


def kernel(**inputs):
    import numpy as _np
    import concourse.bacc as _bacc
    from concourse import mybir as _mybir
    from concourse.bass_utils import run_bass_kernel_spmd as _run

    a = {k: _np.asarray(v) for k, v in inputs.items()}
    pre = "L0_xattn_"
    order = _np.arange(512).reshape(4, 4, 32).transpose(1, 0, 2).ravel()
    a[pre + "Wv"], a[pre + "bv"] = a[pre + "Wv"][:, order], a[pre + "bv"][order]
    a[pre + "Wo"] = a[pre + "Wo"][order]
    cols = [a[pre + n].reshape(-1, 128).T for n in ("bq", "bk", "bv", "gq", "betq", "gkv", "betkv")]
    cols.append(a["L0_ffn_b1"].reshape(-1, 128).T)
    arrays = {
        "x": a["x"], "ctx_in": a["ctx_1024"],
        "w_q": a[pre + "Wq"], "w_k": a[pre + "Wk"], "w_v": a[pre + "Wv"], "w_o": a[pre + "Wo"],
        "w1t": a["L0_ffn_W1"].T, "w2t": a["L0_ffn_W2"].T,
        "cols": _np.concatenate(cols, axis=1),
        "bo": a[pre + "bo"], "b2": a["L0_ffn_b2"], "g_x": a["g_xattn"], "g_f": a["g_ffn"],
    }
    arrays = {k: _np.ascontiguousarray(v) for k, v in arrays.items()}
    nc = _bacc.Bacc("TRN2", target_bir_lowering=False, num_devices=1)
    args = {k: nc.dram_tensor(k, v.shape, _mybir.dt.from_np(v.dtype), kind="ExternalInput").ap()
            for k, v in arrays.items()}
    out = nc.dram_tensor("out", a["x"].shape, _mybir.dt.float32, kind="ExternalOutput").ap()
    gated_block(nc, out=out, **args)
    r = _run(nc, [arrays], core_ids=[0])
    return r.results[0]["out"]
```

```python
from contextlib import ExitStack

import concourse.bass as bass
from concourse import mybir

ALU = mybir.AluOpType
ACT = mybir.ActivationFunctionType
AX = mybir.AxisListType
F32 = mybir.dt.float32
F16 = mybir.dt.float16
F8 = mybir.dt.float8e4

P = 128
B, NQ, NK, D = 8, 224, 750, 512
H, HD = 16, 32
F = 2048
DC = D // P
FC = F // P
KT, KR = 6, 125
KH = NK // 2
QSTART = (0, NQ - P)
QNEW = (0, 2 * P - NQ)
EPS = 1e-5
SPLIT_ROWS = 3 * HD
STACK_ROWS = SPLIT_ROWS + 2
VW = HD + 1

Z_SCALE, W_SCALE, Y_SCALE = 16.0, 64.0, 4.0
QK_SCALE, V_SCALE, M_SCALE = 4.0, 16.0, 16.0
PSUM_TO_QK = QK_SCALE / (Z_SCALE * W_SCALE)
PSUM_TO_V = V_SCALE / (Z_SCALE * W_SCALE)
PSUM_TO_O = 1.0 / (V_SCALE * W_SCALE)
EXP_SCALE = HD ** -0.5 / (QK_SCALE * QK_SCALE)
P_LOG_SCALE = 8.317766166719343
MAX_SHIFT = P_LOG_SCALE / EXP_SCALE / M_SCALE

PIECES = 16
PIECE_RING = 3

NORM = ("stat", "rstd", "norm", "cx", "xx")
PREP = ("q", "k", "v")
FINISH = ("divide", "ot", "bias", "op", "rstd2", "norm2", "yt", "bias2", "f1", "f2")
FILL_KINDS = ("cx", "xx", "q", "k", "v", "mr", "ot", "op", "yt", "f1", "f2")
SLOT_WORK = [
    [("q", 0), ("q", 1), ("mr", 1), ("bias", 0), ("divide", 0), ("k", 0)],
    [("k", 1), ("ot", 0), ("k", 2), ("ot", 1)],
    [("k", 3), ("op", 0), ("rstd2", 0), ("stat", 0), ("mr", 2)],
    [("op", 1), ("stat", 1), ("v", 0)],
    [("v", 1), ("norm2", 0), ("stat", 2), ("k", 4), ("k", 5), ("yt", 0)],
    [("k", 6), ("mr", 3), ("k", 7), ("stat", 3), ("norm2", 1)],
    [("v", 2), ("yt", 1), ("stat", 4), ("stat", 5), ("v", 3)],
    [("f1", 0), ("mr", 4), ("f1", 1)],
    [("f1", 2), ("mr", 5), ("rstd", 0), ("stat", 6), ("stat", 7), ("f1", 3)],
    [("v", 4), ("f1", 4), ("norm", 0), ("norm", 1), ("bias2", 0)],
    [("f1", 5), ("f1", 6), ("norm", 2), ("mr", 6), ("norm", 3), ("v", 5)],
    [("f1", 7), ("cx", 0), ("norm", 4), ("cx", 1), ("norm", 5), ("norm", 6), ("norm", 7)],
    [("f2", 0), ("mr", 7), ("xx", 0)],
    [("f2", 1), ("cx", 2), ("cx", 3)],
    [("f2", 2), ("mr", -1), ("cx", 4)],
    [("f2", 3), ("xx", 1), ("cx", 5)],
]


OPEN, FIRST, SECOND, INNER = (0, 0, 0, 1), (0, 1, 0, 1), (1, 1, 0, 1), (1, 1, 1, 1)
THIRD_LAST, SECOND_LAST, LAST = (1, 1, 1, 0), (1, 0, 1, 0), (0, 0, 1, 0)
ORDER = [OPEN, FIRST, SECOND] + [INNER] * (B - 3) + [THIRD_LAST, SECOND_LAST, LAST]
SET_UP = ("gain", "weight", "bias_sum", "bias_ready", "load_pieces", "piece_sum", "ternary", "reload")
OPEN_WORK = [
    [("stat", 0), ("stat", 1), ("stat", 2), ("stat", 3), ("stat", 4), ("stat", 5), ("stat", 6),
     ("stat", 7), ("rstd", 0), ("gain", 0), ("weight", 0), ("weight", 1), ("weight", 2), ("weight", 3),
     ("weight", 4), ("weight", 5), ("weight", 6), ("weight", 7), ("bias_sum", 0), ("bias_sum", 1),
     ("bias_sum", 2), ("bias_sum", 3), ("load_pieces", 0), ("norm", 0), ("norm", 1), ("cx", 0), ("cx", 1),
     ("norm", 2), ("bias_sum", 4), ("cx", 2), ("norm", 3), ("bias_sum", 5), ("cx", 3), ("norm", 4),
     ("norm", 5), ("bias_sum", 6), ("cx", 4), ("bias_sum", 7), ("cx", 5), ("norm", 6), ("norm", 7),
     ("bias_sum", 8), ("xx", 0), ("bias_sum", 9), ("xx", 1), ("bias_sum", 10), ("bias_sum", 11),
     ("piece_sum", 0), ("bias_ready", 0), ("weight", 8), ("weight", 9), ("weight", 10), ("weight", 11),
     ("piece_sum", 1), ("piece_sum", 2)],
]
FIRST_WORK = [
    [("q", 0), ("piece_sum", 3)],
    [("q", 1), ("weight", 12), ("piece_sum", 4)],
    [("k", 0), ("weight", 13), ("k", 1), ("piece_sum", 5)],
    [("k", 2), ("weight", 14), ("k", 3), ("piece_sum", 6)],
    [("k", 4), ("weight", 15), ("k", 5), ("piece_sum", 7)],
    [("k", 6), ("piece_sum", 8), ("k", 7)],
    [("v", 0), ("stat", 0), ("stat", 1), ("piece_sum", 9)],
    [("v", 1), ("stat", 2), ("stat", 3), ("piece_sum", 10)],
    [("v", 2), ("stat", 4), ("stat", 5), ("piece_sum", 11)],
    [("v", 3), ("stat", 6), ("stat", 7), ("rstd", 0), ("piece_sum", 12)],
    [("v", 4), ("piece_sum", 13)],
    [("norm", 0), ("norm", 1)],
    [("v", 5), ("norm", 2), ("norm", 3), ("piece_sum", 14)],
    [("cx", 0), ("norm", 4), ("cx", 1), ("norm", 5), ("norm", 6), ("norm", 7), ("piece_sum", 15)],
    [("cx", 2), ("cx", 3), ("cx", 4)],
    [("cx", 5), ("mr", -1), ("xx", 0), ("xx", 1)],
]
SECOND_WORK = [
    [("q", 0), ("q", 1), ("ternary", 0), ("mr", 1), ("k", 0)],
    [("k", 1), ("k", 2), ("ternary", 1), ("reload", 0)],
    [("k", 3), ("stat", 0), ("ternary", 2), ("mr", 2), ("reload", 1)],
    [("stat", 1), ("v", 0), ("ternary", 3), ("reload", 2)],
    [("v", 1), ("stat", 2), ("ternary", 4), ("k", 4), ("k", 5), ("reload", 3)],
    [("k", 6), ("mr", 3), ("ternary", 5), ("k", 7), ("stat", 3), ("reload", 4)],
    [("v", 2), ("stat", 4), ("ternary", 6), ("stat", 5), ("v", 3), ("reload", 5)],
    [("mr", 4), ("ternary", 7), ("reload", 6)],
    [("mr", 5), ("rstd", 0), ("ternary", 8), ("stat", 6), ("stat", 7), ("reload", 7)],
    [("v", 4), ("norm", 0), ("ternary", 9), ("norm", 1), ("reload", 8)],
    [("norm", 2), ("mr", 6), ("ternary", 10), ("norm", 3), ("v", 5), ("reload", 9)],
    [("cx", 0), ("norm", 4), ("ternary", 11), ("cx", 1), ("norm", 5), ("norm", 6), ("norm", 7),
     ("reload", 10)],
    [("mr", 7), ("xx", 0), ("ternary", 12), ("reload", 11)],
    [("cx", 2), ("cx", 3), ("ternary", 13), ("reload", 12)],
    [("mr", -1), ("cx", 4), ("ternary", 14)],
    [("xx", 1), ("cx", 5), ("ternary", 15)],
]
WORK = {OPEN: OPEN_WORK + [[]] * (H - 1), FIRST: FIRST_WORK, SECOND: SECOND_WORK}


def slot_steps(slot, attend, prep, finish, norm):
    work = [(k, i) if (prep and (k in PREP or i == -1)) or (finish and k in FINISH) or
            (norm and k in NORM) or (attend and k == "mr" and i > 0) or k in SET_UP else None
            for k, i in WORK.get((attend, prep, finish, norm), SLOT_WORK)[slot]]
    early = prep if slot >= 12 else attend
    pv = attend if slot else finish
    steps = [("score", 0)] * early + [("expo", 0)] * attend + work[0:1]
    steps += [("expo", 1)] * attend + [("score", 1)] * early + work[1:2]
    steps += [("expo", 2)] * attend + [("pv", (slot - 1) % H)] * pv + work[2:]
    return [s for s in steps if s]


def fill_list(stages):
    return [s for slot in range(H) for s in slot_steps(slot, *stages) if s[0] in FILL_KINDS]


def fills_before(b):
    if isinstance(b, int):
        return sum(len(fill_list(stages)) for stages in ORDER[:b + 2])
    inner = len(fill_list(INNER))
    return b * inner + (fills_before(1) - inner)


def gated_block(nc, x, ctx_in, w_q, w_k, w_v, w_o, w1t, w2t, cols, bo, b2, g_x, g_f, out):
    with ExitStack() as ctx:
        def sb(name, shape, dt):
            return ctx.enter_context(nc.sbuf_tensor(name, shape, dt))

        def sem(name):
            return ctx.enter_context(nc.semaphore(name))

        whl = {n: [sb(f"w{n}_{part}", [P, DC, D], F16) for part in ("hi", "lo")] for n in "qkvo"}
        w1q = sb("w1_ternary", [P, DC, F], F8)
        w2q = sb("w2_ternary", [P, FC, D], F8)
        ctx_raw = sb("ctx_raw", [P, KT, D], F32)
        kh = sb("k_stage_hi", [P, DC, NK], F16)
        kl = sb("k_stage_lo", [P, DC, NK], F16)
        qk_full = sb("qk_full", [P, 2, 2 * NQ], F32)
        ctx_t = [sb(f"ctx_t_{part}", [P, DC, NK], F16) for part in ("hi", "lo")]
        x_t = [sb(f"x_t_{part}", [P, DC, NQ], F16) for part in ("hi", "lo")]
        qh = sb("q_stage_hi", [P, DC, NQ], F16)
        ql = sb("q_stage_lo", [P, DC, NQ], F16)
        v_stage = sb("v_stage", [P, KT, H, 2, VW], F16)
        v_flat = sb("v_now", [P, KT * H * 2 * VW], F16)
        v_now = v_flat[:, :].rearrange("p (i h s d) -> p i h s d", i=KT, h=H, s=2)
        k_flat = sb("k_stack", [P, H * NK], F16)
        k_stack = k_flat[:, :].rearrange("p (h n) -> p h n", h=H)
        q_stack = sb("q_stack", [P, H, NQ], F16)
        p_full = sb("p_full", [P, 2, 2 * NQ], F32)
        p_flat = sb("p_parts", [P, 2 * 6 * 2 * NQ], F16)
        p_parts = p_flat[:, :].rearrange("p (s u n) -> p s u n", s=2, u=6)
        ph, pl = p_parts[:, 0], p_parts[:, 1]
        h_flat = sb("h_parts", [P, 2 * FC * NQ], F16)
        h_parts = h_flat[:, :].rearrange("p (s c n) -> p s c n", s=2, c=FC)
        hh, hl = h_parts[:, 0], h_parts[:, 1]
        h_full = sb("h_full", [P, 2, 2 * NQ], F32)
        o_t = [sb(f"o_t_{part}", [P, DC, NQ], F16) for part in ("hi", "lo")]
        xq = sb("x_for_q", [P, 2, D], F32)
        xb = sb("x_residual", [P, 2, D], F32)
        o_sum = sb("o_sum", [P, 2, H, VW], F32)
        yo = sb("rows_to_turn", [P, 2, D], F32)
        bo_row = sb("bo_row", [P, D], F32)
        b2_row = sb("b2_row", [P, D], F32)
        ident = sb("ident", [P, P], F32)
        ident16 = sb("ident16", [P, P], F16)
        ones = sb("ones", [P, P], F32)
        col = sb("columns", [P, 44], F32)
        g2 = sb("gates", [P, 2], F32)
        gt = sb("gates_tanh", [P, 2], F32)
        gains = sb("gains", [P, 10], F32)
        bias = sb("bias", [P, 12], F32)
        bias4 = sb("bias4", [P, 8], F32)
        b1y = sb("b1_scaled", [P, FC], F32)
        bn1 = sb("bn1", [P, 8, 6], F32)
        mv1 = sb("mean_var1", [P, 8, 2], F32)
        r1 = sb("rstd1", [P, 5, 8], F32)
        bn2 = sb("bn2", [P, 2, 6], F32)
        mv2 = sb("mean_var2", [P, 2, 2], F32)
        r2 = sb("rstd2", [P, 5, 2], F32)
        minus_m = sb("minus_m", [48, H * NK // 48], F16)
        minus_half = sb("minus_half", [P, 8], F32)
        mx = sb("row_max", [P, H, 2], F32)
        mxs = sb("row_max_scaled", [P, 2, 2], F32)
        mhl = sb("row_max_parts", [P, H, 2, 2], F16)
        rden = sb("rden", [P, 2, H], F32)
        abs_sum = sb("abs_sum", [P, PIECES], F32)
        abs_tot = sb("abs_tot", [P, 2], F32)
        thr = sb("thresholds", [P, 4], F32)

        raw = {"k": k_flat[:, 0:2 * DC * D], "v": k_flat[:, 2 * DC * D:4 * DC * D],
               "q": v_flat[:, 0:2 * DC * D], "o": p_flat[:, 0:2 * DC * D]}
        raw = {n: a.bitcast(F32).rearrange("p (c n) -> p c n", c=DC) for n, a in raw.items()}
        piece = h_flat[:, 0:PIECE_RING * 2048].bitcast(F32).rearrange("p (r n) -> p r n", r=PIECE_RING)
        below = yo[:, :, :].rearrange("p a b -> p (a b)").bitcast(F16)[:, 0:1024]
        bv_wide = o_sum[:, :, :, :].rearrange("p a b c -> p (a b c)")[:, 0:DC * P]
        bv_wide = bv_wide.rearrange("p (c n) -> p c n", c=DC)

        ps_score = ctx.enter_context(nc.psum_tensor("ps_score", [P, 2, 512], F32))
        ps_exp = ctx.enter_context(nc.psum_tensor("ps_exp", [P, 2, 512], F32))
        ps_pv = ctx.enter_context(nc.psum_tensor("ps_pv", [P, 2, 512], F32))
        ps_fill = ctx.enter_context(nc.psum_tensor("ps_fill", [P, 2, 512], F32))

        ctx_loaded, x_loaded, xb_loaded = sem("ctx_loaded"), sem("x_loaded"), sem("xb_loaded")
        kq_landed = [sem(f"kq_landed{c}") for c in range(DC)]
        v_landed = [sem(f"v_landed{c}") for c in range(DC)]
        out_stored = sem("out_stored")
        w_loaded = {n: sem(f"w{n}_loaded") for n in "qkvo"}
        small_loaded = sem("small_loaded")
        piece_loaded = [sem(f"piece_loaded{r}") for r in range(PIECE_RING)]
        piece_summed, piece_done = sem("piece_summed"), sem("piece_done")
        piece_below = sem("piece_below")
        consts, passed, rows_set = sem("consts"), sem("passed"), sem("rows_set")
        gate_ready, gains_ready = sem("gate_ready"), sem("gains_ready")
        w_hi, w_split = sem("w_hi"), sem("w_split")
        bias_sums, bias_step, wide_ready = sem("bias_sums"), sem("bias_step"), sem("wide_ready")
        bo_sums, bo_step = sem("bo_sums"), sem("bo_step")
        tot_ready, tot_all, thr_step = sem("tot_ready"), sem("tot_all"), sem("thr_step")
        fill_ready = sem("fill_ready")
        scores_ready, max_taken = sem("scores_ready"), sem("max_taken")
        max_scaled, max_hi, max_split = sem("max_scaled"), sem("max_hi"), sem("max_split")
        shift_rows = sem("shift_rows")
        logits_ready, exp_done, p_split = sem("logits_ready"), sem("exp_done"), sem("p_split")
        pv_done, o_taken = sem("pv_done"), sem("o_taken")
        o_recip, o_normed = sem("o_recip"), sem("o_normed")
        stats1_step, stats1, rstd1_step = sem("stats1_step"), sem("stats1"), sem("rstd1_step")
        ctx_normed, x_normed = sem("ctx_normed"), sem("x_normed")
        stats2_step, stats2, rstd2_step = sem("stats2_step"), sem("stats2"), sem("rstd2_step")
        norm1_ready, norm2_ready = sem("norm1_ready"), sem("norm2_ready")
        y_normed = sem("y_normed")
        ctx_hi, ctx_split = sem("ctx_hi"), sem("ctx_split")
        x_hi, x_split = sem("x_hi"), sem("x_split")
        qk_lifted, qk_hi, qk_split = sem("qk_lifted"), sem("qk_hi"), sem("qk_split")
        v_hi, v_split = sem("v_hi"), sem("v_split")
        o_hi, o_split = sem("o_hi"), sem("o_split")
        xb_biased, x1_ready, x1_biased = sem("xb_biased"), sem("x1_ready"), sem("x1_biased")
        y_hi, y_split = sem("y_hi"), sem("y_split")
        h_lifted, h_hi, h_split = sem("h_lifted"), sem("h_hi"), sem("h_split")
        out_ready = sem("out_ready")

        FREED = {"cx": (ctx_split, 6, 0), "xx": (x_split, 2, 0), "q": (qk_lifted, 10, 0),
                 "k": (qk_lifted, 10, 2), "v": (v_split, 6, 0), "mr": (shift_rows, 8, 0),
                 "ot": (o_split, 2, 0), "op": (x1_ready, 2, 0), "yt": (y_split, 2, 0),
                 "f1": (h_lifted, 8, 0), "f2": (out_ready, 4, 4)}

        def batch_of(kind, i, b):
            return b + 2 if kind in NORM else b + 1 if kind in PREP or i == -1 else \
                b - 1 if kind in FINISH else b

        def freed(kind, i, b):
            s, per_batch, first = FREED[kind]
            return s, batch_of(kind, i, b) * per_batch + (first + max(i, 0) + 1)

        block = ctx.enter_context(nc.Block())

        def wait_alone(eng, s, value):
            eng.wait_ge(s, value)
            eng.sem_inc(passed, 1)

        def iterations(eng, body):
            body(0, SECOND)
            with eng.Fori(1, B - 2) as b:
                body(b, INNER)
            body(B - 2, THIRD_LAST)
            body(B - 1, SECOND_LAST)
            body(B, LAST)

        def q_cols(t):
            return slice(QNEW[t], P), slice(QSTART[t] + QNEW[t], QSTART[t] + P)

        @block.sync
        def _(sp):
            def load_ctx(n):
                sp.dma_start(ctx_raw[0:KR, :, :], ctx_in[n].rearrange("(i p) d -> p i d", p=KR)) \
                    .then_inc(ctx_loaded, 16)

            def load_x(n, dst, loaded):
                for t in range(2):
                    sp.dma_start(dst[:, t, :], x[n][QSTART[t]:QSTART[t] + P, :]).then_inc(loaded, 16)

            def copy_kq(g):
                for part, (ks, qs) in enumerate(((kh, qh), (kh, ql), (kl, qh))):
                    for stack, stage in ((q_stack, qs), (k_stack, ks)):
                        sp.dma_start(stack[HD * part:HD * part + HD, 4 * g:4 * g + 4, :],
                                     stage[HD * g:HD * g + HD, :, :]).then_inc(kq_landed[g], 16)

            def copy_v(c):
                sp.dma_start(v_now[0:KR, :, 4 * c:4 * c + 4], v_stage[0:KR, :, 4 * c:4 * c + 4]) \
                    .then_inc(v_landed[c], 16)

            def body(b, stages):
                attend, prep, finish, norm = stages
                n = b + 1
                if finish:
                    wait_alone(sp, out_stored, b * 32)
                    load_x(b - 1, xb, xb_loaded)
                if norm and stages != OPEN:
                    wait_alone(sp, ctx_split, n * 6 + 6)
                    load_ctx(n + 1)
                    wait_alone(sp, x_split, n * 2 + 2)
                    load_x(n + 1, xq, x_loaded)
                if attend:
                    if finish:
                        wait_alone(sp, pv_done, b * 16)
                    copy_v(3)
                if prep:
                    wait_alone(sp, qk_split, n * 10 + 10)
                    for c in range(DC):
                        if attend:
                            wait_alone(sp, logits_ready, b * 48 + 12 * (c + 1))
                        copy_kq(c)
                        if c == 1:
                            wait_alone(sp, v_split, n * 6 + 6)
                        if c >= 1:
                            if attend:
                                wait_alone(sp, pv_done, b * 16 + 4 * c)
                            copy_v(c - 1)
                if finish:
                    wait_alone(sp, out_ready, b * 4 + 4)
                    for t in range(2):
                        rows, to = q_cols(t)
                        sp.dma_start(out[b - 1][to, :], xb[rows, t, :]).then_inc(out_stored, 16)
            load_x(0, xq, x_loaded)
            load_ctx(0)
            sp.sem_inc(out_stored, 32)
            for a, b_ in ((col[:, :], cols), (g2[:, 0:1], g_x.partition_broadcast(P)),
                          (g2[:, 1:2], g_f.partition_broadcast(P)),
                          (bo_row[:, :], bo.partition_broadcast(P)), (b2_row[:, :], b2.partition_broadcast(P))):
                sp.dma_start(a, b_).then_inc(small_loaded, 16)
            for name, w in (("q", w_q), ("k", w_k), ("v", w_v), ("o", w_o)):
                sp.dma_start(raw[name], w.rearrange("(c p) n -> p c n", p=P)).then_inc(w_loaded[name], 16)
            sp.wait_ge(w_split, 3 * DC)
            sp.wait_ge(bias_sums, 3 * DC)
            sp.wait_ge(consts, 7)
            for row in range(SPLIT_ROWS, STACK_ROWS):
                sp.dma_start(k_flat[row:row + 1, :], minus_m[:, :]).then_inc(rows_set, 16)
            body(-1, FIRST)
            iterations(sp, body)
            sp.wait_ge(out_stored, B * 32 + 32)

        def load_piece(eng, k):
            k16 = k % PIECES
            if k16 < 8:
                src = w1t[(k16 // 2) * P:(k16 // 2 + 1) * P, (k16 % 2) * 1024:(k16 % 2 + 1) * 1024]
                dst = piece[:, k % PIECE_RING, :]
            else:
                src = w2t[(k16 - 8) * 2 * P:(k16 - 7) * 2 * P, :].rearrange("(c p) n -> p c n", p=P)
                dst = piece[:, k % PIECE_RING, :].rearrange("p (c n) -> p c n", c=2)
            eng.dma_start(dst, src).then_inc(piece_loaded[k % PIECE_RING], 16)

        @block.tensor
        def _(pe):
            def three(out_ap, left, right, order=((0, 0), (0, 1), (1, 0)), chunks=DC):
                n = 0
                for c in range(chunks):
                    for a, b_ in order:
                        last = pe.matmul(out_ap, left(a, c), right(b_, c), start=(n == 0),
                                         stop=(n == chunks * len(order) - 1))
                        n += 1
                return last

            def score(n, h, t):
                if t == 0 and h % 4 == 0:
                    pe.wait_ge(kq_landed[h // 4], n * 96 + 96)
                if not (isinstance(n, int) and n == 0 and h + t == 0):
                    pe.wait_ge(max_taken, n * 32 + (2 * h + t))
                for half in range(2):
                    last = pe.matmul(ps_score[:, half, 0:KH],
                                     q_stack[0:SPLIT_ROWS, h, QSTART[t]:QSTART[t] + P],
                                     k_stack[0:SPLIT_ROWS, h, half * KH:half * KH + KH],
                                     start=True, stop=True)
                last.then_inc(scores_ready, 1)

            def expo(b, h, u):
                if u == 0 and h % 2 == 0:
                    pe.wait_ge(shift_rows, b * 8 + (h // 2 + 1))
                if not (isinstance(b, int) and b * 48 + 3 * h + u < 2):
                    pe.wait_ge(exp_done, b * 48 + (3 * h + u - 1))
                for kt in (2 * u, 2 * u + 1):
                    last = pe.matmul(ps_exp[0:KR, (3 * h + u) % 2, (kt % 2) * NQ:(kt % 2) * NQ + NQ],
                                     k_stack[0:STACK_ROWS, h, kt * KR:kt * KR + KR],
                                     q_stack[0:STACK_ROWS, h, :], start=True, stop=True)
                last.then_inc(logits_ready, 1)

            def pv(b, h):
                if h % 4 == 0:
                    pe.wait_ge(v_landed[h // 4], b * 16 + 16)
                pe.wait_ge(p_split, b * 48 + (3 * h + 3))
                if not (isinstance(b, int) and b * 16 + h < 2):
                    pe.wait_ge(o_taken, b * 16 + (h - 1))
                for t in range(2):
                    for kt in range(KT):
                        for part in (ph, pl):
                            q0 = (kt % 2) * NQ + QSTART[t]
                            last = pe.matmul(
                                ps_pv[:, h % 2, t * 2 * VW:(t + 1) * 2 * VW],
                                part[0:KR, 3 * (h % 2) + kt // 2, q0:q0 + P],
                                v_now[0:KR, kt, h].rearrange("p a b -> p (a b)"),
                                start=(kt == 0 and part is ph), stop=(kt == KT - 1 and part is pl))
                last.then_inc(pv_done, 1)

            def turn(rows, bank, src, size=P):
                for c in range(DC):
                    last = pe.transpose(ps_fill[:, bank, c * size:(c + 1) * size],
                                        src[0:rows, c * P:(c + 1) * P], ident[0:rows, 0:rows])
                return last

            def fill(kind, i, b, bank):
                n, p_ = b + 1, b - 1
                if kind == "cx":
                    pe.wait_ge(ctx_normed, (b + 2) * 6 + (i + 1))
                    last = turn(KR, bank, ctx_raw[:, i, :], KR)
                elif kind == "xx":
                    pe.wait_ge(x_normed, (b + 2) * 2 + (i + 1))
                    last = turn(P, bank, xq[:, i, :])
                elif kind == "q":
                    if i == 0:
                        pe.wait_ge(x_split, n * 2 + 2)
                        if isinstance(b, int) and b == -1:
                            pe.wait_ge(w_split, DC)
                    for j in range(2):
                        m = slice((2 * i + j) * P, (2 * i + j + 1) * P)
                        last = three(ps_fill[:, bank, j * NQ:(j + 1) * NQ],
                                     lambda a, c: whl["q"][a][:, c, m], lambda a, c: x_t[a][:, c, :])
                elif kind == "k":
                    if i == 0:
                        pe.wait_ge(ctx_split, n * 6 + 6)
                        if isinstance(b, int) and b == -1:
                            pe.wait_ge(w_split, 2 * DC)
                    m, r = slice((i // 2) * P, (i // 2 + 1) * P), slice((i % 2) * KH, (i % 2 + 1) * KH)
                    last = three(ps_fill[:, bank, 0:KH], lambda a, c: whl["k"][a][:, c, m],
                                 lambda a, c: ctx_t[a][:, c, r])
                elif kind == "v":
                    if i == 0 and isinstance(b, int) and b == -1:
                        pe.wait_ge(w_split, 3 * DC)
                    r = slice(i * KR, (i + 1) * KR)
                    last = three(ps_fill[0:KR, bank, :], lambda a, c: ctx_t[a][:, c, r],
                                 lambda a, c: whl["v"][a][:, c, :])
                elif kind == "mr":
                    m, nb = (i, b) if i > 0 else (0, n)
                    pe.wait_ge(max_split, nb * 8 + (m + 1))
                    for h in (2 * m, 2 * m + 1):
                        for t in range(2):
                            frm, to = q_cols(t)
                            last = pe.matmul(
                                ps_fill[SPLIT_ROWS:STACK_ROWS, bank, (h % 2) * NQ + to.start:(h % 2) * NQ + to.stop],
                                mhl[:, h, t, :], ident16[:, frm], start=True, stop=True,
                                tile_position=(0, SPLIT_ROWS))
                elif kind == "ot":
                    pe.wait_ge(o_normed, p_ * 2 + (i + 1))
                    last = turn(P, bank, yo[:, i, :])
                elif kind == "op":
                    if i == 0:
                        pe.wait_ge(o_split, p_ * 2 + 2)
                    last = three(ps_fill[:, bank, :], lambda a, c: o_t[a][:, c, QSTART[i]:QSTART[i] + P],
                                 lambda a, c: whl["o"][a][:, c, :])
                elif kind == "yt":
                    pe.wait_ge(y_normed, p_ * 2 + (i + 1))
                    last = turn(P, bank, yo[:, i, :])
                elif kind == "f1":
                    if i == 0:
                        wait_alone(pe, y_split, p_ * 2 + 2)
                        if not isinstance(b, int):
                            pe.wait_ge(piece_done, PIECES)
                    for j in range(2):
                        m = slice((2 * i + j) * P, (2 * i + j + 1) * P)
                        last = three(ps_fill[:, bank, j * NQ:(j + 1) * NQ], lambda a, c: w1q[:, c, m],
                                     lambda a, c: o_t[a][:, c, :], order=((0, 0), (0, 1)))
                else:
                    if i == 0:
                        wait_alone(pe, h_split, p_ * 8 + 8)
                    t, w = i // 2, slice((i % 2) * 256, (i % 2 + 1) * 256)
                    r = slice(QSTART[t], QSTART[t] + P)
                    last = three(ps_fill[:, bank, 0:256], lambda a, c: (hh, hl)[a][:, c, r],
                                 lambda a, c: w2q[:, c, w], order=((0, 0), (1, 0)), chunks=FC)
                last.then_inc(fill_ready, 1)

            def bias_sum(j):
                name, beta = (("q", 16), ("k", 24), ("v", 24))[j // DC]
                if j == 0:
                    pe.wait_ge(small_loaded, 80)
                if j % DC == 0:
                    pe.wait_ge(w_loaded[name], 16)
                m = slice(j % DC * P, (j % DC + 1) * P)
                for c in range(DC):
                    last = pe.matmul(ps_pv[:, 0, j:j + 1], raw[name][:, c, m], col[:, beta + c:beta + c + 1],
                                     start=(c == 0), stop=(c == DC - 1))
                last.then_inc(bias_sums, 1)

            def before(stages):
                return ORDER[ORDER.index(stages) - 1]

            def body(b, stages):
                done = []
                if stages != OPEN:
                    last_two = fill_list(before(stages))[-2:] + (fill_list(INNER)[-2:] if stages == INNER else [])
                    for s, value in {freed(*f, b - 1)[0].name: freed(*f, b - 1) for f in last_two}.values():
                        pe.wait_ge(s, value)
                for slot in range(H):
                    for kind, i in slot_steps(slot, *stages):
                        if kind == "score":
                            h = (slot + 4) % H
                            score(b + 1 if slot >= 12 else b, h, i)
                        elif kind == "expo":
                            expo(b, slot, i)
                        elif kind == "pv":
                            pv(b if slot else b - 1, i)
                        elif kind == "bias_sum":
                            bias_sum(i)
                        elif kind in FILL_KINDS:
                            if len(done) >= 2:
                                if kind in ("f1", "f2"):
                                    wait_alone(pe, *freed(*done[-2], b))
                                else:
                                    pe.wait_ge(*freed(*done[-2], b))
                            fill(kind, i, b, len(done) % 2)
                            done.append((kind, i))

            pe.wait_ge(consts, 5)
            body(-2, OPEN)
            body(-1, FIRST)
            pe.wait_ge(wide_ready, DC)
            for c in range(DC):
                last = pe.matmul(ps_pv[:, 1, :], bv_wide[:, c, :], raw["o"][:, c, :],
                                 start=(c == 0), stop=(c == DC - 1))
            last.then_inc(bo_sums, 1)
            pe.wait_ge(tot_ready, 2)
            pe.matmul(ps_pv[:, 0, 0:2], ones[:, :], abs_tot[:, :], start=True, stop=True).then_inc(tot_all, 1)
            pe.wait_ge(thr_step, 1)
            pe.wait_ge(rows_set, 32)
            iterations(pe, body)

        @block.scalar
        def _(act):
            def expo(b, h, u):
                k = 3 * h + u
                act.wait_ge(logits_ready, b * 48 + (k + 1))
                if not (isinstance(b, int) and b * 48 + k < 2):
                    act.wait_ge(p_split, b * 48 + (k - 1))
                if u == 0 and not (isinstance(b, int) and b * 16 + h < 2):
                    act.wait_ge(pv_done, b * 16 + (h - 1))
                unit = 3 * (h % 2) + u
                nc.scalar.activation(p_full[0:KR, k % 2, :], ps_exp[0:KR, k % 2, 0:2 * NQ], ACT.Exp,
                                     scale=EXP_SCALE)
                nc.scalar.activation(ph[0:KR, unit, :], ps_exp[0:KR, k % 2, 0:2 * NQ], ACT.Exp,
                                     scale=EXP_SCALE).then_inc(exp_done, 1)

            def fill(kind, i, b, bank, ready):
                n, p_ = b + 1, b - 1
                if kind in ("op", "f2"):
                    return
                act.wait_ge(fill_ready, ready)
                if kind == "cx":
                    nc.scalar.activation(ctx_t[0][:, :, i * KR:(i + 1) * KR],
                                         ps_fill[:, bank, 0:DC * KR].rearrange("p (c n) -> p c n", c=DC),
                                         ACT.Copy, scale=Z_SCALE).then_inc(ctx_hi, 1)
                elif kind in ("xx", "ot", "yt"):
                    dst, scale, s = {"xx": (x_t, Z_SCALE, x_hi), "ot": (o_t, 1.0, o_hi),
                                     "yt": (o_t, Y_SCALE, y_hi)}[kind]
                    frm, to = q_cols(i)
                    src = ps_fill[:, bank, :].rearrange("p (c n) -> p c n", c=DC)[:, :, frm]
                    nc.scalar.activation(dst[0][:, :, to], src, ACT.Copy, scale=scale).then_inc(s, 1)
                elif kind == "q":
                    if isinstance(b, int) and b == -1 and i == 0:
                        act.wait_ge(bias_step, 3)
                    if not (isinstance(b, int) and b == -1):
                        act.wait_ge(qk_split, n * 10 + (i - 1))
                    for j in range(2):
                        last = nc.scalar.activation(qk_full[:, i % 2, j * NQ:(j + 1) * NQ],
                                                    ps_fill[:, bank, j * NQ:(j + 1) * NQ], ACT.Identity,
                                                    bias=bias4[:, 2 * i + j:2 * i + j + 1], scale=PSUM_TO_QK)
                    last.then_inc(qk_lifted, 1)
                elif kind == "k":
                    act.wait_ge(qk_split, n * 10 + (i + 1))
                    nc.scalar.activation(qk_full[:, i % 2, 0:KH], ps_fill[:, bank, 0:KH], ACT.Identity,
                                         bias=bias4[:, 4 + i // 2:5 + i // 2],
                                         scale=PSUM_TO_QK).then_inc(qk_lifted, 1)
                elif kind == "v":
                    if i == 0 and not (isinstance(b, int) and b == -1):
                        act.wait_ge(v_landed[3], n * 16)
                    nc.scalar.activation(v_stage[0:KR, i, :, 0, 0:HD],
                                         ps_fill[0:KR, bank, :].rearrange("p (h d) -> p h d", h=H),
                                         ACT.Copy, scale=PSUM_TO_V).then_inc(v_hi, 1)
                elif kind == "mr":
                    m = max(i, 0)
                    nc.scalar.activation(q_stack[SPLIT_ROWS:STACK_ROWS, 2 * m:2 * m + 2, :],
                                         ps_fill[SPLIT_ROWS:STACK_ROWS, bank, 0:2 * NQ]
                                         .rearrange("p (h n) -> p h n", h=2), ACT.Copy).then_inc(shift_rows, 1)
                elif kind == "f1":
                    if i >= 2:
                        act.wait_ge(h_split, p_ * 8 + (i - 1))
                    for j in range(2):
                        last = nc.scalar.activation(h_full[:, i % 2, j * NQ:(j + 1) * NQ],
                                                    ps_fill[:, bank, j * NQ:(j + 1) * NQ], ACT.Relu,
                                                    bias=b1y[:, 2 * i + j:2 * i + j + 1])
                    last.then_inc(h_lifted, 1)

            def norm(n, j):
                if j == 0:
                    act.wait_ge(norm1_ready, n + 1)
                if j < KT:
                    nc.scalar.activation(ctx_raw[0:KR, j, :], ctx_raw[0:KR, j, :], ACT.Identity,
                                         bias=r1[0:KR, 4, j:j + 1], scale=r1[0:KR, 3, j:j + 1]) \
                        .then_inc(ctx_normed, 1)
                else:
                    nc.scalar.activation(xq[:, j - KT, :], xq[:, j - KT, :], ACT.Identity,
                                         bias=r1[:, 4, j:j + 1], scale=r1[:, 3, j:j + 1]) \
                        .then_inc(x_normed, 1)

            def norm2(p_, t):
                if t == 0:
                    act.wait_ge(norm2_ready, p_ + 1)
                    act.wait_ge(o_split, p_ * 2 + 2)
                nc.scalar.activation(yo[:, t, :], xb[:, t, :], ACT.Identity, bias=r2[:, 4, t:t + 1],
                                     scale=r2[:, 3, t:t + 1]).then_inc(y_normed, 1)

            def weight_hi(k):
                name, at = (("q", 0), ("k", 4), ("v", 4), ("o", 8))[k // DC]
                c = k % DC
                if k == 0:
                    act.wait_ge(gains_ready, 4)
                if c == 0:
                    act.wait_ge(w_loaded[name], 16)
                at += 0 if name == "o" else c
                nc.scalar.activation(whl[name][0][:, c, :], raw[name][:, c, :], ACT.Copy,
                                     scale=gains[:, at:at + 1]).then_inc(w_hi, 1)

            def sum_piece(k):
                act.wait_ge(piece_loaded[k % PIECE_RING], 16 * (k // PIECE_RING + 1))
                nc.scalar.activation(piece[:, k % PIECE_RING, :], piece[:, k % PIECE_RING, :], ACT.Abs,
                                     accum_out=abs_sum[:, k:k + 1]).then_inc(piece_summed, 1)
                act.wait_ge(piece_summed, k + 1)
                load_piece(act, k + PIECE_RING)

            def body(b, stages):
                done = 0
                for slot in range(H):
                    for kind, i in slot_steps(slot, *stages):
                        if kind == "expo":
                            expo(b, slot, i)
                        elif kind == "norm":
                            norm(b + 2, i)
                        elif kind == "weight":
                            weight_hi(i)
                        elif kind == "load_pieces":
                            act.wait_ge(w_loaded["v"], 16)
                            for k in range(PIECE_RING):
                                load_piece(act, k)
                        elif kind == "piece_sum":
                            sum_piece(i)
                        elif kind == "reload":
                            act.wait_ge(piece_done, i + 1)
                            load_piece(act, PIECES + i + PIECE_RING)
                        elif kind == "norm2":
                            norm2(b - 1, i)
                        elif kind in FILL_KINDS:
                            fill(kind, i, b, done % 2, fills_before(b) + (done + 1))
                            done += 1

            act.wait_ge(small_loaded, 80)
            nc.scalar.activation(gt[:, :], g2[:, :], ACT.Tanh).then_inc(gate_ready, 1)
            body(-2, OPEN)
            body(-1, FIRST)
            act.wait_ge(w_split, 4 * DC)
            act.wait_ge(bo_sums, 1)
            iterations(act, body)

        @block.vector
        def _(dve):
            def score(n, h, t):
                dve.wait_ge(scores_ready, n * 32 + (2 * h + t + 1))
                nc.vector.tensor_reduce(mx[:, h, t:t + 1], ps_score[:, :, 0:KH], AX.XY, ALU.max) \
                    .then_inc(max_taken, 1)

            def split_max(n, m):
                dve.wait_ge(max_taken, n * 32 + (4 * m + 4))
                nc.vector.tensor_scalar(mxs[:, :, :], mx[:, 2 * m:2 * m + 2, :], 1.0 / M_SCALE, -MAX_SHIFT,
                                        ALU.mult, ALU.add).then_inc(max_scaled, 1)
                dve.wait_ge(max_scaled, n * 8 + (m + 1))
                nc.vector.tensor_copy(mhl[:, 2 * m:2 * m + 2, :, 0], mxs[:, :, :]).then_inc(max_hi, 1)
                dve.wait_ge(max_hi, n * 8 + (m + 1))
                nc.vector.tensor_tensor(mhl[:, 2 * m:2 * m + 2, :, 1], mxs[:, :, :],
                                        mhl[:, 2 * m:2 * m + 2, :, 0], ALU.subtract).then_inc(max_split, 1)

            def expo(b, h, u):
                k, unit = 3 * h + u, 3 * (h % 2) + u
                dve.wait_ge(exp_done, b * 48 + (k + 1))
                nc.vector.tensor_tensor(pl[0:KR, unit, :], p_full[0:KR, k % 2, :], ph[0:KR, unit, :],
                                        ALU.subtract).then_inc(p_split, 1)

            def take_o(b, h):
                dve.wait_ge(pv_done, b * 16 + (h + 1))
                if h == 0 and not (isinstance(b, int) and b == 0):
                    dve.wait_ge(o_normed, b * 2)
                nc.vector.tensor_reduce(o_sum[:, :, h, :],
                                        ps_pv[:, h % 2, 0:4 * VW].rearrange("p (t s d) -> p t d s", t=2, s=2),
                                        AX.X, ALU.add).then_inc(o_taken, 1)

            def divide(b):
                dve.wait_ge(o_taken, b * 16 + 16)
                nc.vector.reciprocal(rden[:, :, :], o_sum[:, :, :, HD]).then_inc(o_recip, 1)
                dve.wait_ge(o_recip, b + 1)
                for t in range(2):
                    nc.vector.tensor_tensor(yo[:, t, :].rearrange("p (h d) -> p h d", h=H),
                                            o_sum[:, t, :, 0:HD],
                                            rden[:, t, :].unsqueeze(2).to_broadcast([P, H, HD]),
                                            ALU.mult).then_inc(o_normed, 1)

            def stat(n, j):
                if j == 0:
                    dve.wait_ge(ctx_loaded, n * 16 + 16)
                if j == KT:
                    dve.wait_ge(x_loaded, n * 32 + 32)
                if j < KT:
                    nc.vector.bn_stats(bn1[0:KR, j, :], ctx_raw[0:KR, j, :]).then_inc(stats1_step, 1)
                else:
                    nc.vector.bn_stats(bn1[:, j, :], xq[:, j - KT, :]).then_inc(stats1_step, 1)
                if j == KT + 1:
                    if not (isinstance(n, int) and n == 0):
                        wait_alone(dve, x_normed, n * 2)
                    wait_alone(dve, stats1_step, n * 8 + 8)
                    for i in range(KT):
                        nc.vector.bn_aggr(mv1[0:KR, i, :], bn1[0:KR, i, :])
                    for i in range(KT, KT + 2):
                        last = nc.vector.bn_aggr(mv1[:, i, :], bn1[:, i, :])
                    last.then_inc(stats1, 1)

            def stats_finish(p_):
                for t in range(2):
                    dve.wait_ge(x1_ready, p_ * 2 + (t + 1))
                    last = nc.vector.bn_stats(bn2[:, t, :], xb[:, t, :])
                last.then_inc(stats2_step, 1)
                wait_alone(dve, stats2_step, p_ + 1)
                for t in range(2):
                    last = nc.vector.bn_aggr(mv2[:, t, :], bn2[:, t, :])
                last.then_inc(stats2, 1)

            def fill(kind, i, b, bank, ready):
                n, p_ = b + 1, b - 1
                if kind == "cx":
                    dve.wait_ge(ctx_hi, (b + 2) * 6 + (i + 1))
                    r = slice(i * KR, (i + 1) * KR)
                    nc.vector.scalar_tensor_tensor(
                        ctx_t[1][:, :, r], ps_fill[:, bank, 0:DC * KR].rearrange("p (c n) -> p c n", c=DC),
                        Z_SCALE, ctx_t[0][:, :, r], ALU.mult, ALU.subtract).then_inc(ctx_split, 1)
                elif kind in ("xx", "ot", "yt"):
                    dst, scale, hi, s = {"xx": (x_t, Z_SCALE, x_hi, x_split), "ot": (o_t, 1.0, o_hi, o_split),
                                         "yt": (o_t, Y_SCALE, y_hi, y_split)}[kind]
                    dve.wait_ge(hi, (b + 2 if kind == "xx" else p_) * 2 + (i + 1))
                    frm, to = q_cols(i)
                    src = ps_fill[:, bank, :].rearrange("p (c n) -> p c n", c=DC)[:, :, frm]
                    nc.vector.scalar_tensor_tensor(dst[1][:, :, to], src, scale, dst[0][:, :, to],
                                                   ALU.mult, ALU.subtract).then_inc(s, 1)
                elif kind == "q":
                    if i == 0 and not (isinstance(b, int) and b == -1):
                        for g in range(4):
                            dve.wait_ge(kq_landed[g], n * 96)
                    dve.wait_ge(qk_lifted, n * 10 + (i + 1))
                    nc.vector.tensor_copy(qh[:, 2 * i:2 * i + 2, :],
                                          qk_full[:, i % 2, 0:2 * NQ].rearrange("p (c n) -> p c n", c=2)) \
                        .then_inc(qk_hi, 1)
                elif kind == "k":
                    dve.wait_ge(qk_lifted, n * 10 + (i + 3))
                    nc.vector.tensor_copy(kh[:, i // 2, (i % 2) * KH:(i % 2 + 1) * KH],
                                          qk_full[:, i % 2, 0:KH]).then_inc(qk_hi, 1)
                elif kind == "v":
                    dve.wait_ge(v_hi, n * 6 + (i + 1))
                    nc.vector.scalar_tensor_tensor(
                        v_stage[0:KR, i, :, 1, 0:HD], ps_fill[0:KR, bank, :].rearrange("p (h d) -> p h d", h=H),
                        PSUM_TO_V, v_stage[0:KR, i, :, 0, 0:HD], ALU.mult, ALU.subtract).then_inc(v_split, 1)
                elif kind == "op":
                    dve.wait_ge(fill_ready, ready)
                    dve.wait_ge(xb_biased, p_ * 2 + (i + 1))
                    nc.vector.scalar_tensor_tensor(xb[:, i, :], ps_fill[:, bank, :], PSUM_TO_O, xb[:, i, :],
                                                   ALU.mult, ALU.add).then_inc(x1_ready, 1)
                    if i == 1:
                        stats_finish(p_)
                elif kind == "f1":
                    dve.wait_ge(h_lifted, p_ * 8 + (i + 1))
                    nc.vector.tensor_copy(hh[:, 2 * i:2 * i + 2, :],
                                          h_full[:, i % 2, :].rearrange("p (c n) -> p c n", c=2)) \
                        .then_inc(h_hi, 1)
                elif kind == "f2":
                    dve.wait_ge(fill_ready, ready)
                    dve.wait_ge(x1_biased, p_ * 2 + (i // 2 + 1))
                    w = slice((i % 2) * 256, (i % 2 + 1) * 256)
                    nc.vector.scalar_tensor_tensor(xb[:, i // 2, w], ps_fill[:, bank, 0:256], gains[:, 9:10],
                                                   xb[:, i // 2, w], ALU.mult, ALU.add).then_inc(out_ready, 1)

            def gain():
                dve.wait_ge(small_loaded, 80)
                nc.vector.tensor_scalar(gains[:, 0:4], col[:, 12:16], W_SCALE, None, ALU.mult).then_inc(gains_ready, 1)
                nc.vector.tensor_scalar(gains[:, 4:8], col[:, 20:24], W_SCALE, None, ALU.mult).then_inc(gains_ready, 1)
                dve.wait_ge(gate_ready, 1)
                nc.vector.tensor_scalar(gains[:, 8:9], gt[:, 0:1], W_SCALE, None, ALU.mult).then_inc(gains_ready, 1)
                nc.vector.tensor_scalar(gains[:, 9:10], gt[:, 1:2], 1.0 / Y_SCALE, None, ALU.mult) \
                    .then_inc(gains_ready, 1)
                nc.vector.tensor_scalar(b1y[:, :], col[:, 28:44], Y_SCALE, None, ALU.mult)
                nc.vector.tensor_scalar(b2_row[:, :], b2_row[:, :], gt[:, 1:2], None, ALU.mult).then_inc(bo_step, 1)
                dve.wait_ge(gains_ready, 4)

            def weight_lo(k):
                name, at = (("q", 0), ("k", 4), ("v", 4), ("o", 8))[k // DC]
                c = k % DC
                at += 0 if name == "o" else c
                dve.wait_ge(w_hi, k + 1)
                nc.vector.scalar_tensor_tensor(whl[name][1][:, c, :], raw[name][:, c, :], gains[:, at:at + 1],
                                               whl[name][0][:, c, :], ALU.mult, ALU.subtract).then_inc(w_split, 1)

            def bias_ready():
                dve.wait_ge(bias_sums, 3 * DC)
                nc.vector.tensor_tensor(bias[:, :], ps_pv[:, 0, 0:12], col[:, 0:12], ALU.add).then_inc(bias_step, 1)
                dve.wait_ge(bias_step, 1)
                nc.vector.tensor_scalar(bias4[:, :], bias[:, 0:8], QK_SCALE, None, ALU.mult).then_inc(bias_step, 2)
                for c in range(DC):
                    nc.vector.tensor_scalar(bv_wide[:, c, :], ones[:, :], bias[:, 8 + c:9 + c], None,
                                            ALU.mult).then_inc(wide_ready, 1)

            def quantise(k):
                j = k // 8
                kk = PIECES + k
                src = piece[:, kk % PIECE_RING, :]
                dst = w1q[:, k // 2, (k % 2) * 1024:(k % 2 + 1) * 1024] if k < 8 else \
                    w2q[:, 2 * (k - 8):2 * (k - 8) + 2, :].rearrange("p c n -> p (c n)")
                dve.wait_ge(piece_loaded[kk % PIECE_RING], 16 * (kk // PIECE_RING + 1))
                if k:
                    dve.wait_ge(piece_done, k)
                nc.vector.tensor_scalar(below, src, thr[:, 2 + j:3 + j], None, ALU.is_lt).then_inc(piece_below, 1)
                dve.wait_ge(piece_below, k + 1)
                nc.vector.scalar_tensor_tensor(dst, src, thr[:, j:j + 1], below, ALU.is_gt, ALU.subtract,
                                               saturate=False) \
                    .then_inc(piece_done, 1)

            def body(b, stages):
                done = 0
                attend, prep, finish, norm = stages
                for slot in range(H):
                    m = slot // 2 + 1
                    if slot % 2 == 0 and (prep if m == H // 2 else attend):
                        split_max(b if m < H // 2 else b + 1, m % (H // 2))
                    for kind, i in slot_steps(slot, *stages):
                        if kind == "score":
                            score(b + 1 if slot >= 12 else b, (slot + 4) % H, i)
                        elif kind == "expo":
                            if i:
                                expo(b, slot, i - 1)
                            elif slot:
                                expo(b, slot - 1, 2)
                            elif stages != SECOND:
                                expo(b - 1, H - 1, 2)
                        elif kind == "pv":
                            take_o(b if slot else b - 1, i)
                        elif kind == "stat":
                            stat(b + 2, i)
                        elif kind == "gain":
                            gain()
                        elif kind == "weight":
                            weight_lo(i)
                        elif kind == "bias_ready":
                            bias_ready()
                        elif kind == "ternary":
                            quantise(i)
                        elif kind == "divide":
                            divide(b - 1)
                        elif kind in FILL_KINDS:
                            fill(kind, i, b, done % 2, fills_before(b) + (done + 1))
                            done += 1
                if stages == SECOND_LAST:
                    expo(b, H - 1, 2)

            dve.wait_ge(consts, 5)
            nc.vector.memset(thr[:, :], 0.0).then_inc(out_ready, 4)
            body(-2, OPEN)
            body(-1, FIRST)
            dve.wait_ge(bo_sums, 1)
            nc.vector.tensor_tensor(bo_row[:, :], ps_pv[:, 1, :], bo_row[:, :], ALU.add).then_inc(bo_step, 1)
            dve.wait_ge(bo_step, 2)
            nc.vector.tensor_scalar(bo_row[:, :], bo_row[:, :], gt[:, 0:1], None, ALU.mult).then_inc(bo_step, 1)
            dve.wait_ge(piece_summed, PIECES)
            for j in range(2):
                nc.vector.tensor_reduce(abs_tot[:, j:j + 1], abs_sum[:, 8 * j:8 * j + 8], AX.X, ALU.add) \
                    .then_inc(tot_ready, 1)
            dve.wait_ge(tot_all, 1)
            nc.vector.tensor_scalar(thr[:, 0:2], ps_pv[:, 0, 0:2], 0.5 / (D * F), 0.5 * EPS, ALU.mult, ALU.add) \
                .then_inc(thr_step, 1)
            dve.wait_ge(thr_step, 1)
            nc.vector.tensor_scalar(thr[:, 2:4], thr[:, 0:2], -1.0, None, ALU.mult).then_inc(thr_step, 1)
            dve.wait_ge(thr_step, 2)
            iterations(dve, body)

        @block.gpsimd
        def _(pool):
            def rstd(r, step, base, width, mean, done):
                nc.gpsimd.tensor_tensor(r[:, 1, :], r[:, 0, :], minus_half[:, 0:width], ALU.pow).then_inc(step, 1)
                pool.wait_ge(step, base + 1)
                nc.gpsimd.tensor_tensor(r[:, 2, :], r[:, 1, :], r[:, 1, :], ALU.mult).then_inc(step, 1)
                pool.wait_ge(step, base + 2)
                nc.gpsimd.tensor_tensor(r[:, 2, :], r[:, 2, :], r[:, 0, :], ALU.mult).then_inc(step, 1)
                wait_alone(pool, step, base + 3)
                nc.gpsimd.tensor_scalar(r[:, 2, :], r[:, 2, :], -0.5, 1.5, ALU.mult, ALU.add).then_inc(step, 1)
                pool.wait_ge(step, base + 4)
                nc.gpsimd.tensor_tensor(r[:, 3, :], r[:, 1, :], r[:, 2, :], ALU.mult).then_inc(step, 1)
                pool.wait_ge(step, base + 5)
                nc.gpsimd.tensor_tensor(r[:, 4, :], mean, r[:, 3, :], ALU.mult).then_inc(step, 1)
                wait_alone(pool, step, base + 6)
                nc.gpsimd.tensor_scalar(r[:, 4, :], r[:, 4, :], -1.0, None, ALU.mult).then_inc(done, 1)

            def rstd_prep(n):
                wait_alone(pool, stats1, n + 1)
                nc.gpsimd.tensor_scalar(r1[:, 0, 0:KT], mv1[:, 0:KT, 1], EPS, None, ALU.add).then_inc(rstd1_step, 1)
                nc.gpsimd.tensor_scalar(r1[:, 0, KT:8], mv1[:, KT:8, 1], 1.0 + EPS, EPS * EPS, ALU.mult, ALU.add) \
                    .then_inc(rstd1_step, 1)
                pool.wait_ge(rstd1_step, n * 8 + 2)
                rstd(r1, rstd1_step, n * 8 + 2, 8, mv1[:, :, 0], norm1_ready)

            def rstd_finish(p_):
                wait_alone(pool, stats2, p_ + 1)
                nc.gpsimd.tensor_scalar(r2[:, 0, :], mv2[:, :, 1], EPS, None, ALU.add).then_inc(rstd2_step, 1)
                pool.wait_ge(rstd2_step, p_ * 7 + 1)
                rstd(r2, rstd2_step, p_ * 7 + 1, 2, mv2[:, :, 0], norm2_ready)

            def bias_x1(p_):
                pool.wait_ge(y_normed, p_ * 2 + 2)
                for t in range(2):
                    nc.gpsimd.tensor_tensor(xb[:, t, :], xb[:, t, :], b2_row[:, :], ALU.add).then_inc(x1_biased, 1)

            def bias_residual(p_):
                pool.wait_ge(xb_loaded, p_ * 32 + 32)
                for t in range(2):
                    nc.gpsimd.tensor_tensor(xb[:, t, :], xb[:, t, :], bo_row[:, :], ALU.add).then_inc(xb_biased, 1)

            def fill(kind, i, b):
                n, p_ = b + 1, b - 1
                if kind == "q":
                    pool.wait_ge(qk_hi, n * 10 + (i + 1))
                    nc.gpsimd.tensor_tensor(ql[:, 2 * i:2 * i + 2, :],
                                            qk_full[:, i % 2, 0:2 * NQ].rearrange("p (c n) -> p c n", c=2),
                                            qh[:, 2 * i:2 * i + 2, :], ALU.subtract).then_inc(qk_split, 1)
                elif kind == "k":
                    pool.wait_ge(qk_hi, n * 10 + (i + 3))
                    r = slice((i % 2) * KH, (i % 2 + 1) * KH)
                    nc.gpsimd.tensor_tensor(kl[:, i // 2, r], qk_full[:, i % 2, 0:KH], kh[:, i // 2, r],
                                            ALU.subtract).then_inc(qk_split, 1)
                elif kind == "f1":
                    pool.wait_ge(h_hi, p_ * 8 + (i + 1))
                    nc.gpsimd.tensor_tensor(hl[:, 2 * i:2 * i + 2, :],
                                            h_full[:, i % 2, :].rearrange("p (c n) -> p c n", c=2),
                                            hh[:, 2 * i:2 * i + 2, :], ALU.subtract).then_inc(h_split, 1)

            def body(b, stages):
                for slot in range(H):
                    for kind, i in slot_steps(slot, *stages):
                        if kind == "bias":
                            bias_residual(b - 1)
                        elif kind == "rstd":
                            rstd_prep(b + 2)
                        elif kind == "rstd2":
                            rstd_finish(b - 1)
                        elif kind == "bias2":
                            bias_x1(b - 1)
                        else:
                            fill(kind, i, b)

            nc.gpsimd.memset(ident[:, :], 0.0).then_inc(consts, 1)
            pool.wait_ge(consts, 1)
            nc.gpsimd.affine_select(out=ident[:, :], in_=ident[:, :], compare_op=ALU.not_equal, fill=1.0,
                                    base=0, pattern=[[-1, P]], channel_multiplier=1).then_inc(consts, 1)
            pool.wait_ge(consts, 2)
            nc.gpsimd.tensor_copy(ident16[:, :], ident[:, :]).then_inc(consts, 1)
            nc.gpsimd.memset(ones[:, :], 1.0).then_inc(consts, 1)
            nc.gpsimd.memset(minus_half[:, :], -0.5)
            nc.gpsimd.memset(mv1[:, :, :], 1.0)
            nc.gpsimd.memset(v_stage[:, :, :, :, HD:VW], 0.0).then_inc(consts, 1)
            pool.wait_ge(consts, 5)
            nc.gpsimd.memset(v_stage[:, :, :, 0, HD:VW], 1.0).then_inc(consts, 1)
            nc.gpsimd.memset(minus_m[:, :], -M_SCALE).then_inc(consts, 1)
            body(-2, OPEN)
            body(-1, FIRST)
            pool.wait_ge(bo_step, 3)
            iterations(pool, body)


def kernel(**inputs):
    import numpy as _np
    import concourse.bacc as _bacc
    from concourse import mybir as _mybir
    from concourse.bass_utils import run_bass_kernel_spmd as _run

    a = {k: _np.asarray(v) for k, v in inputs.items()}
    pre = "L0_xattn_"
    order = _np.arange(512).reshape(4, 4, 32).transpose(1, 0, 2).ravel()
    a[pre + "Wv"], a[pre + "bv"] = a[pre + "Wv"][:, order], a[pre + "bv"][order]
    a[pre + "Wo"] = a[pre + "Wo"][order]
    cols = [a[pre + n].reshape(-1, 128).T for n in ("bq", "bk", "bv", "gq", "betq", "gkv", "betkv")]
    cols.append(a["L0_ffn_b1"].reshape(-1, 128).T)
    arrays = {
        "x": a["x"], "ctx_in": a["ctx_1024"],
        "w_q": a[pre + "Wq"], "w_k": a[pre + "Wk"], "w_v": a[pre + "Wv"], "w_o": a[pre + "Wo"],
        "w1t": a["L0_ffn_W1"].T, "w2t": a["L0_ffn_W2"].T,
        "cols": _np.concatenate(cols, axis=1),
        "bo": a[pre + "bo"], "b2": a["L0_ffn_b2"], "g_x": a["g_xattn"], "g_f": a["g_ffn"],
    }
    arrays = {k: _np.ascontiguousarray(v) for k, v in arrays.items()}
    nc = _bacc.Bacc("TRN2", target_bir_lowering=False, num_devices=1)
    args = {k: nc.dram_tensor(k, v.shape, _mybir.dt.from_np(v.dtype), kind="ExternalInput").ap()
            for k, v in arrays.items()}
    out = nc.dram_tensor("out", a["x"].shape, _mybir.dt.float32, kind="ExternalOutput").ap()
    gated_block(nc, out=out, **args)
    r = _run(nc, [arrays], core_ids=[0])
    return r.results[0]["out"]
```

```python
from contextlib import ExitStack

import concourse.bass as bass
from concourse import mybir

ALU = mybir.AluOpType
ACT = mybir.ActivationFunctionType
AX = mybir.AxisListType
F32 = mybir.dt.float32
F16 = mybir.dt.float16
F8 = mybir.dt.float8e4

P = 128
B, NQ, NK, D = 8, 224, 750, 512
H, HD = 16, 32
F = 2048
DC = D // P
FC = F // P
KT, KR = 6, 125
KH = NK // 2
QSTART = (0, NQ - P)
QNEW = (0, 2 * P - NQ)
EPS = 1e-5
SPLIT_ROWS = 3 * HD
MAX_END = SPLIT_ROWS + 2
STACK_ROWS = MAX_END + 1
VW = HD + 1

Z_SCALE, W_SCALE, Y_SCALE = 16.0, 64.0, 4.0
QK_SCALE, V_SCALE, M_SCALE = 4.0, 16.0, 16.0
PSUM_TO_QK = QK_SCALE / (Z_SCALE * W_SCALE)
PSUM_TO_V = V_SCALE / (Z_SCALE * W_SCALE)
PSUM_TO_O = 1.0 / (V_SCALE * W_SCALE)
EXP_SCALE = HD ** -0.5 / (QK_SCALE * QK_SCALE)
SHIFT = 47.0

PIECES = 16
PIECE_RING = 3

NORM = ("stat", "rstd", "norm", "cx", "xx")
PREP = ("q", "k", "v")
FINISH = ("divide", "ot", "bias", "op", "rstd2", "norm2", "yt", "bias2", "f1", "f2")
FILL_KINDS = ("cx", "xx", "q", "k", "v", "mr", "ot", "op", "yt", "f1", "f2")
SLOT_WORK = [
    [("q", 0), ("q", 1), ("mr", 1), ("bias", 0), ("divide", 0), ("k", 0)],
    [("k", 1), ("ot", 0), ("k", 2), ("ot", 1)],
    [("k", 3), ("op", 0), ("rstd2", 0), ("stat", 0), ("mr", 2)],
    [("op", 1), ("stat", 1), ("v", 0)],
    [("v", 1), ("norm2", 0), ("stat", 2), ("k", 4), ("k", 5), ("yt", 0)],
    [("k", 6), ("mr", 3), ("k", 7), ("stat", 3), ("norm2", 1)],
    [("v", 2), ("yt", 1), ("stat", 4), ("stat", 5), ("v", 3)],
    [("f1", 0), ("mr", 4), ("f1", 1)],
    [("f1", 2), ("mr", 5), ("rstd", 0), ("stat", 6), ("stat", 7), ("f1", 3)],
    [("v", 4), ("f1", 4), ("norm", 0), ("norm", 1), ("bias2", 0)],
    [("f1", 5), ("f1", 6), ("norm", 2), ("mr", 6), ("norm", 3), ("v", 5)],
    [("f1", 7), ("cx", 0), ("norm", 4), ("cx", 1), ("norm", 5), ("norm", 6), ("norm", 7)],
    [("f2", 0), ("mr", 7), ("xx", 0)],
    [("f2", 1), ("cx", 2), ("cx", 3)],
    [("f2", 2), ("mr", -1), ("cx", 4)],
    [("f2", 3), ("xx", 1), ("cx", 5)],
]


OPEN, FIRST, SECOND, INNER = (0, 0, 0, 1), (0, 1, 0, 1), (1, 1, 0, 1), (1, 1, 1, 1)
THIRD_LAST, SECOND_LAST, LAST = (1, 1, 1, 0), (1, 0, 1, 0), (0, 0, 1, 0)
ORDER = [OPEN, FIRST, SECOND] + [INNER] * (B - 3) + [THIRD_LAST, SECOND_LAST, LAST]
SET_UP = ("gain", "weight", "bias_sum", "bias_ready", "load_pieces", "piece_sum", "tot", "bo_sum",
          "threshold", "ternary", "reload")
OPEN_WORK = [
    [("stat", 0), ("stat", 1), ("stat", 2), ("stat", 3), ("stat", 4), ("stat", 5), ("stat", 6),
     ("stat", 7), ("rstd", 0), ("gain", 0), ("weight", 0), ("weight", 1), ("weight", 2), ("weight", 3),
     ("weight", 4), ("weight", 5), ("weight", 6), ("weight", 7), ("bias_sum", 0), ("bias_sum", 1),
     ("load_pieces", 0), ("norm", 0), ("norm", 1), ("cx", 0), ("cx", 1), ("bias_sum", 2), ("norm", 2),
     ("norm", 3), ("cx", 2), ("cx", 3), ("norm", 4), ("norm", 5), ("piece_sum", 0), ("cx", 4), ("cx", 5),
     ("norm", 6), ("norm", 7), ("piece_sum", 1), ("xx", 0), ("xx", 1), ("bias_ready", 0),
     ("piece_sum", 2), ("weight", 8), ("weight", 9), ("weight", 10), ("weight", 11)],
]
FIRST_WORK = [
    [("q", 0), ("piece_sum", 3)],
    [("q", 1), ("weight", 12), ("piece_sum", 4)],
    [("k", 0), ("piece_sum", 5), ("weight", 13), ("k", 1)],
    [("k", 2), ("piece_sum", 6), ("weight", 14), ("k", 3)],
    [("k", 4), ("stat", 0), ("piece_sum", 7), ("weight", 15), ("k", 5), ("stat", 1)],
    [("k", 6), ("stat", 2), ("piece_sum", 8), ("k", 7), ("stat", 3)],
    [("v", 0), ("stat", 4), ("stat", 5), ("piece_sum", 9)],
    [("v", 1), ("stat", 6), ("stat", 7), ("rstd", 0), ("piece_sum", 10)],
    [("v", 2), ("piece_sum", 11), ("norm", 0), ("norm", 1)],
    [("norm", 2), ("norm", 3)],
    [],
    [],
    [("v", 3), ("norm", 4), ("bo_sum", 0), ("piece_sum", 12)],
    [("v", 4), ("norm", 5), ("piece_sum", 13)],
    [("v", 5), ("norm", 6), ("cx", 0), ("norm", 7), ("cx", 1), ("piece_sum", 14)],
    [("cx", 2), ("cx", 3), ("mr", -1), ("cx", 4), ("piece_sum", 15), ("tot", 0), ("cx", 5), ("xx", 0),
     ("threshold", 0), ("xx", 1)],
]
SECOND_WORK = [
    [],
    [("mr", 1), ("ternary", 0)],
    [("q", 0), ("mr", 2), ("ternary", 1), ("q", 1), ("stat", 0), ("stat", 1), ("reload", 0), ("k", 0),
     ("stat", 2), ("k", 1), ("ternary", 2), ("k", 2), ("stat", 3), ("reload", 1)],
    [("v", 0), None, ("ternary", 3), ("reload", 2), ("v", 1), ("stat", 4), ("k", 3)],
    [("k", 4), None, ("ternary", 4), ("stat", 5), ("mr", 3), ("k", 5), ("reload", 3)],
    [("k", 6), None, ("reload", 4), ("ternary", 5)],
    [("k", 7), ("ternary", 6), ("stat", 6), ("stat", 7), ("ternary", 7), ("mr", 4), ("v", 2), ("rstd", 0),
     ("reload", 5)],
    [("v", 3)],
    [None, ("reload", 6), ("mr", 5), ("norm", 0), ("ternary", 8), ("reload", 7), ("norm", 1)],
    [("v", 4), ("ternary", 9), ("v", 5), ("norm", 2), ("norm", 3), ("reload", 8)],
    [("ternary", 10), ("cx", 0), ("norm", 4), ("reload", 9), ("reload", 10), ("ternary", 11), ("norm", 5),
     ("cx", 1)],
    [("cx", 2), None, ("mr", 6), ("ternary", 12), ("cx", 3)],
    [("mr", 7), ("norm", 6), ("ternary", 13), ("reload", 11)],
    [("norm", 7)],
    [("xx", 0), ("cx", 4), ("mr", -1), ("reload", 12)],
    [("ternary", 14), ("cx", 5), ("xx", 1), ("ternary", 15)],
]
SECOND_LAST_WORK = [
    [None, None, ("mr", 1), ("divide", 0)],
    [("ot", 0), ("ot", 1)],
    [("op", 0), ("op", 1), ("bias", 0), ("rstd2", 0), ("mr", 2)],
    [None, None, ("norm2", 0)],
    [("yt", 0), None, ("mr", 3), ("norm2", 1)],
    [("bias2", 0), ("yt", 1)],
    [("f1", 0), None, ("mr", 4)],
    [("f1", 1), None, ("f1", 2)],
    [("f1", 3), ("f1", 4), ("mr", 5)],
    [("f1", 5), None, ("f1", 6)],
    [("f1", 7)],
    [("mr", 6), None, ("f2", 0)],
    [None, ("f2", 1), ("mr", 7)],
    [None, ("f2", 2)],
    [],
    [None, ("f2", 3)],
]
LAST_WORK = [
    [None, None, ("divide", 0), ("ot", 0), ("ot", 1), ("bias", 0), ("op", 0), ("op", 1), ("rstd2", 0),
     ("norm2", 0), ("norm2", 1), ("yt", 0), ("yt", 1), ("f1", 0), ("f1", 1), ("f1", 2), ("f1", 3),
     ("f1", 4), ("f1", 5), ("f1", 6), ("f1", 7), ("bias2", 0), ("f2", 0), ("f2", 1), ("f2", 2), ("f2", 3)],
]
WORK = {OPEN: OPEN_WORK + [[]] * (H - 1), FIRST: FIRST_WORK, SECOND: SECOND_WORK,
        LAST: LAST_WORK + [[]] * (H - 1),
        SECOND_LAST: SECOND_LAST_WORK}


def slot_steps(slot, attend, prep, finish, norm):
    work = [step if step and ((prep and (step[0] in PREP or step[1] == -1)) or (finish and step[0] in FINISH)
                              or (norm and step[0] in NORM) or (attend and step[0] == "mr" and step[1] > 0)
                              or step[0] in SET_UP) else None
            for step in WORK.get((attend, prep, finish, norm), SLOT_WORK)[slot]]
    early = prep if slot >= 12 else attend
    pv = attend if slot else finish
    steps = [("score", 0)] * early + [("expo", 0)] * attend + work[0:1]
    steps += [("expo", 1)] * attend + [("score", 1)] * early + work[1:2]
    steps += [("expo", 2)] * attend + [("pv", (slot - 1) % H)] * pv + work[2:]
    return [s for s in steps if s]


def fill_list(stages):
    return [s for slot in range(H) for s in slot_steps(slot, *stages) if s[0] in FILL_KINDS]


def fills_before(b):
    if isinstance(b, int):
        return sum(len(fill_list(stages)) for stages in ORDER[:b + 2])
    inner = len(fill_list(INNER))
    return b * inner + (fills_before(1) - inner)


def gated_block(nc, x, ctx_in, w_q, w_k, w_v, w_o, w1t, w2t, cols, bo, b2, g_x, g_f, out):
    with ExitStack() as ctx:
        def sb(name, shape, dt):
            return ctx.enter_context(nc.sbuf_tensor(name, shape, dt))

        def sem(name):
            return ctx.enter_context(nc.semaphore(name))

        whl = {n: [sb(f"w{n}_{part}", [P, DC, D], F16) for part in ("hi", "lo")] for n in "qkvo"}
        w1q = sb("w1_ternary", [P, DC, F], F8)
        w2q = sb("w2_ternary", [P, FC, D], F8)
        ctx_raw = sb("ctx_raw", [P, KT, D], F32)
        kh = sb("k_stage_hi", [P, DC, NK], F16)
        kl = sb("k_stage_lo", [P, DC, NK], F16)
        qk_full = sb("qk_full", [P, 2, 2 * NQ], F32)
        ctx_t = [sb(f"ctx_t_{part}", [P, DC, NK], F16) for part in ("hi", "lo")]
        x_t = [sb(f"x_t_{part}", [P, DC, NQ], F16) for part in ("hi", "lo")]
        qh = sb("q_stage_hi", [P, DC, NQ], F16)
        ql = sb("q_stage_lo", [P, DC, NQ], F16)
        v_stage = sb("v_stage", [P, KT, H, 2, VW], F16)
        v_flat = sb("v_now", [P, KT * H * 2 * VW], F16)
        v_now = v_flat[:, :].rearrange("p (i h s d) -> p i h s d", i=KT, h=H, s=2)
        k_flat = sb("k_stack", [P, H * NK], F16)
        k_stack = k_flat[:, :].rearrange("p (h n) -> p h n", h=H)
        q_stack = sb("q_stack", [P, H, NQ], F16)
        p_full = sb("p_full", [P, 2, 2 * NQ], F32)
        p_flat = sb("p_parts", [P, 2 * 6 * 2 * NQ], F16)
        p_parts = p_flat[:, :].rearrange("p (s u n) -> p s u n", s=2, u=6)
        ph, pl = p_parts[:, 0], p_parts[:, 1]
        h_flat = sb("h_parts", [P, 2 * FC * NQ], F16)
        h_parts = h_flat[:, :].rearrange("p (s c n) -> p s c n", s=2, c=FC)
        hh, hl = h_parts[:, 0], h_parts[:, 1]
        h_full = sb("h_full", [P, 2, 2 * NQ], F32)
        o_t = [sb(f"o_t_{part}", [P, DC, NQ], F16) for part in ("hi", "lo")]
        xq = sb("x_for_q", [P, 2, D], F32)
        xb = sb("x_residual", [P, 2, D], F32)
        o_sum = sb("o_sum", [P, 2, H, VW], F32)
        yo = sb("rows_to_turn", [P, 2, D], F32)
        bo_row = sb("bo_row", [P, D], F32)
        b2_row = sb("b2_row", [P, D], F32)
        ident = sb("ident", [P, P], F32)
        ident16 = sb("ident16", [P, P], F16)
        ones = sb("ones", [P, P], F32)
        col = sb("columns", [P, 44], F32)
        g2 = sb("gates", [P, 2], F32)
        gt = sb("gates_tanh", [P, 2], F32)
        gains = sb("gains", [P, 10], F32)
        bias = sb("bias", [P, 12], F32)
        bias4 = sb("bias4", [P, 8], F32)
        b1y = sb("b1_scaled", [P, FC], F32)
        bn1 = sb("bn1", [P, 8, 6], F32)
        mv1 = sb("mean_var1", [P, 8, 2], F32)
        r1 = sb("rstd1", [P, 5, 8], F32)
        bn2 = sb("bn2", [P, 2, 6], F32)
        mv2 = sb("mean_var2", [P, 2, 2], F32)
        r2 = sb("rstd2", [P, 5, 2], F32)
        minus_m = sb("minus_m", [48, H * NK // 48], F16)
        minus_half = sb("minus_half", [P, 8], F32)
        mx = sb("row_max", [P, H, 2], F32)
        mhl = sb("row_max_parts", [P, H, 2, 2], F16)
        rden = sb("rden", [P, 2, H], F32)
        abs_sum = sb("abs_sum", [P, PIECES], F32)
        abs_tot = sb("abs_tot", [P, 2], F32)
        thr = sb("thresholds", [P, 4], F32)

        raw = {"k": k_flat[:, 0:2 * DC * D], "v": k_flat[:, 2 * DC * D:4 * DC * D],
               "q": v_flat[:, 0:2 * DC * D], "o": p_flat[:, 0:2 * DC * D]}
        raw = {n: a.bitcast(F32).rearrange("p (c n) -> p c n", c=DC) for n, a in raw.items()}
        piece = h_flat[:, 0:PIECE_RING * 2048].bitcast(F32).rearrange("p (r n) -> p r n", r=PIECE_RING)
        above, below = (yo[:, j, :].bitcast(F16) for j in range(2))
        bias_rows = q_stack[0:1, :, :].rearrange("p h n -> p (h n)")[:, 0:2 * 12 * P].bitcast(F32)
        bv_wide = o_sum[:, :, :, :].rearrange("p a b c -> p (a b c)")[:, 0:DC * P]
        bv_wide = bv_wide.rearrange("p (c n) -> p c n", c=DC)

        ps_score = ctx.enter_context(nc.psum_tensor("ps_score", [P, 2, 512], F32))
        ps_exp = ctx.enter_context(nc.psum_tensor("ps_exp", [P, 2, 512], F32))
        ps_pv = ctx.enter_context(nc.psum_tensor("ps_pv", [P, 2, 512], F32))
        ps_fill = ctx.enter_context(nc.psum_tensor("ps_fill", [P, 2, 512], F32))

        ps_bias = [ps_pv[0:1, 0, :], ps_pv[0:1, 1, :], ps_score[0:1, 0, :]]

        ctx_loaded, x_loaded, xb_loaded = sem("ctx_loaded"), sem("x_loaded"), sem("xb_loaded")
        kq_landed = [sem(f"kq_landed{c}") for c in range(DC)]
        v_landed = [sem(f"v_landed{c}") for c in range(DC)]
        out_stored = sem("out_stored")
        w_loaded = {n: sem(f"w{n}_loaded") for n in "qkvo"}
        small_loaded = sem("small_loaded")
        piece_loaded = [sem(f"piece_loaded{r}") for r in range(PIECE_RING)]
        piece_summed, piece_done = sem("piece_summed"), sem("piece_done")
        piece_compared = sem("piece_compared")
        consts, passed, rows_set = sem("consts"), sem("passed"), sem("rows_set")
        gate_ready, gains_ready = sem("gate_ready"), sem("gains_ready")
        bias_row_ready, bias_turned = sem("bias_row_ready"), sem("bias_turned")
        w_hi, w_split = sem("w_hi"), sem("w_split")
        bias_sums, bias_step, wide_ready = sem("bias_sums"), sem("bias_step"), sem("wide_ready")
        bo_sums, bo_step = sem("bo_sums"), sem("bo_step")
        tot_ready, tot_all, thr_step = sem("tot_ready"), sem("tot_all"), sem("thr_step")
        fill_ready = sem("fill_ready")
        scores_ready, max_taken = sem("scores_ready"), sem("max_taken")
        max_hi, max_split = sem("max_hi"), sem("max_split")
        shift_rows = sem("shift_rows")
        logits_ready, exp_done, p_split = sem("logits_ready"), sem("exp_done"), sem("p_split")
        pv_done, o_taken = sem("pv_done"), sem("o_taken")
        o_recip, o_normed = sem("o_recip"), sem("o_normed")
        stats1_step, stats1, rstd1_step = sem("stats1_step"), sem("stats1"), sem("rstd1_step")
        ctx_normed, x_normed = sem("ctx_normed"), sem("x_normed")
        stats2_step, stats2, rstd2_step = sem("stats2_step"), sem("stats2"), sem("rstd2_step")
        norm1_ready, norm2_ready = sem("norm1_ready"), sem("norm2_ready")
        y_normed = sem("y_normed")
        ctx_hi, ctx_split = sem("ctx_hi"), sem("ctx_split")
        x_hi, x_split = sem("x_hi"), sem("x_split")
        qk_lifted, qk_hi, qk_split = sem("qk_lifted"), sem("qk_hi"), sem("qk_split")
        v_hi, v_split = sem("v_hi"), sem("v_split")
        o_hi, o_split = sem("o_hi"), sem("o_split")
        xb_biased, x1_ready, x1_biased = sem("xb_biased"), sem("x1_ready"), sem("x1_biased")
        y_hi, y_split = sem("y_hi"), sem("y_split")
        h_lifted, h_hi, h_split = sem("h_lifted"), sem("h_hi"), sem("h_split")
        out_ready = sem("out_ready")

        FREED = {"cx": (ctx_split, 6, 0), "xx": (x_split, 2, 0), "q": (qk_lifted, 10, 0),
                 "k": (qk_lifted, 10, 2), "v": (v_split, 6, 0), "mr": (shift_rows, 8, 0),
                 "ot": (o_split, 2, 0), "op": (x1_ready, 2, 0), "yt": (y_split, 2, 0),
                 "f1": (h_lifted, 8, 0), "f2": (out_ready, 4, 4)}

        def batch_of(kind, i, b):
            return b + 2 if kind in NORM else b + 1 if kind in PREP or i == -1 else \
                b - 1 if kind in FINISH else b

        def freed(kind, i, b):
            s, per_batch, first = FREED[kind]
            return s, batch_of(kind, i, b) * per_batch + (first + max(i, 0) + 1)

        block = ctx.enter_context(nc.Block())

        def wait_alone(eng, s, value):
            eng.wait_ge(s, value)
            eng.sem_inc(passed, 1)

        def iterations(eng, body):
            body(0, SECOND)
            with eng.Fori(1, B - 2) as b:
                body(b, INNER)
            body(B - 2, THIRD_LAST)
            body(B - 1, SECOND_LAST)
            body(B, LAST)

        def q_cols(t):
            return slice(QNEW[t], P), slice(QSTART[t] + QNEW[t], QSTART[t] + P)

        @block.sync
        def _(sp):
            def load_ctx(n):
                sp.dma_start(ctx_raw[0:KR, :, :], ctx_in[n].rearrange("(i p) d -> p i d", p=KR)) \
                    .then_inc(ctx_loaded, 16)

            def load_x(n, dst, loaded):
                for t in range(2):
                    sp.dma_start(dst[:, t, :], x[n][QSTART[t]:QSTART[t] + P, :]).then_inc(loaded, 16)

            def copy_kq(g):
                for part, (ks, qs) in enumerate(((kh, qh), (kh, ql), (kl, qh))):
                    for stack, stage in ((q_stack, qs), (k_stack, ks)):
                        sp.dma_start(stack[HD * part:HD * part + HD, 4 * g:4 * g + 4, :],
                                     stage[HD * g:HD * g + HD, :, :]).then_inc(kq_landed[g], 16)

            def copy_v(c):
                sp.dma_start(v_now[0:KR, :, 4 * c:4 * c + 4], v_stage[0:KR, :, 4 * c:4 * c + 4]) \
                    .then_inc(v_landed[c], 16)

            def body(b, stages):
                attend, prep, finish, norm = stages
                n = b + 1
                if finish:
                    wait_alone(sp, out_stored, b * 32)
                    load_x(b - 1, xb, xb_loaded)
                if norm and stages != OPEN:
                    wait_alone(sp, ctx_split, n * 6 + 6)
                    load_ctx(n + 1)
                    wait_alone(sp, x_split, n * 2 + 2)
                    load_x(n + 1, xq, x_loaded)
                if attend:
                    if finish:
                        wait_alone(sp, pv_done, b * 16)
                    copy_v(3)
                if prep:
                    wait_alone(sp, qk_split, n * 10 + 10)
                    for c in range(DC):
                        if attend:
                            wait_alone(sp, logits_ready, b * 48 + 12 * (c + 1))
                        copy_kq(c)
                        if c == 1:
                            wait_alone(sp, v_split, n * 6 + 6)
                        if c >= 1:
                            if attend:
                                wait_alone(sp, pv_done, b * 16 + 4 * c)
                            copy_v(c - 1)
                if finish:
                    wait_alone(sp, out_ready, b * 4 + 4)
                    for t in range(2):
                        rows, to = q_cols(t)
                        sp.dma_start(out[b - 1][to, :], xb[rows, t, :]).then_inc(out_stored, 16)
            load_x(0, xq, x_loaded)
            load_ctx(0)
            sp.sem_inc(out_stored, 32)
            for a, b_ in ((col[:, :], cols), (g2[:, 0:1], g_x.partition_broadcast(P)),
                          (g2[:, 1:2], g_f.partition_broadcast(P)),
                          (bo_row[:, :], bo.partition_broadcast(P)), (b2_row[:, :], b2.partition_broadcast(P))):
                sp.dma_start(a, b_).then_inc(small_loaded, 16)
            for name, w in (("q", w_q), ("k", w_k), ("v", w_v), ("o", w_o)):
                sp.dma_start(raw[name], w.rearrange("(c p) n -> p c n", p=P)).then_inc(w_loaded[name], 16)
            sp.wait_ge(bias_row_ready, 3)
            sp.dma_start(bias[:, :], bias_rows).then_inc(bias_turned, 16)
            sp.wait_ge(w_split, 3 * DC)
            sp.wait_ge(consts, 8)
            for row in range(SPLIT_ROWS, STACK_ROWS):
                sp.dma_start(k_flat[row:row + 1, :], minus_m[:, :]).then_inc(rows_set, 16)
            body(-1, FIRST)
            iterations(sp, body)
            sp.wait_ge(out_stored, B * 32 + 32)

        def load_piece(eng, k):
            k16 = k % PIECES
            if k16 < 8:
                src = w1t[(k16 // 2) * P:(k16 // 2 + 1) * P, (k16 % 2) * 1024:(k16 % 2 + 1) * 1024]
                dst = piece[:, k % PIECE_RING, :]
            else:
                src = w2t[(k16 - 8) * 2 * P:(k16 - 7) * 2 * P, :].rearrange("(c p) n -> p c n", p=P)
                dst = piece[:, k % PIECE_RING, :].rearrange("p (c n) -> p c n", c=2)
            eng.dma_start(dst, src).then_inc(piece_loaded[k % PIECE_RING], 16)

        @block.tensor
        def _(pe):
            def three(out_ap, left, right, order=((0, 0), (0, 1), (1, 0)), chunks=DC, ready=None):
                n = 0
                for c in range(chunks):
                    if ready:
                        ready(c)
                    for a, b_ in order:
                        last = pe.matmul(out_ap, left(a, c), right(b_, c), start=(n == 0),
                                         stop=(n == chunks * len(order) - 1))
                        n += 1
                return last

            def score(n, h, t):
                if t == 0 and h % 4 == 0:
                    pe.wait_ge(kq_landed[h // 4], n * 96 + 96)
                if not (isinstance(n, int) and n == 0 and h + t == 0):
                    pe.wait_ge(max_taken, n * 32 + (2 * h + t))
                for half in range(2):
                    last = pe.matmul(ps_score[:, half, 0:KH],
                                     q_stack[0:SPLIT_ROWS, h, QSTART[t]:QSTART[t] + P],
                                     k_stack[0:SPLIT_ROWS, h, half * KH:half * KH + KH],
                                     start=True, stop=True)
                last.then_inc(scores_ready, 1)

            def expo(b, h, u):
                if u == 0 and h % 2 == 0:
                    pe.wait_ge(shift_rows, b * 8 + (h // 2 + 1))
                if not (isinstance(b, int) and b * 48 + 3 * h + u < 2):
                    pe.wait_ge(exp_done, b * 48 + (3 * h + u - 1))
                for kt in (2 * u, 2 * u + 1):
                    last = pe.matmul(ps_exp[0:KR, (3 * h + u) % 2, (kt % 2) * NQ:(kt % 2) * NQ + NQ],
                                     k_stack[0:STACK_ROWS, h, kt * KR:kt * KR + KR],
                                     q_stack[0:STACK_ROWS, h, :], start=True, stop=True)
                last.then_inc(logits_ready, 1)

            def pv(b, h):
                if h % 4 == 0:
                    pe.wait_ge(v_landed[h // 4], b * 16 + 16)
                pe.wait_ge(p_split, b * 48 + (3 * h + 3))
                if not (isinstance(b, int) and b * 16 + h < 2):
                    pe.wait_ge(o_taken, b * 16 + (h - 1))
                for t in range(2):
                    for kt in range(KT):
                        for part in (ph, pl):
                            q0 = (kt % 2) * NQ + QSTART[t]
                            last = pe.matmul(
                                ps_pv[:, h % 2, t * 2 * VW:(t + 1) * 2 * VW],
                                part[0:KR, 3 * (h % 2) + kt // 2, q0:q0 + P],
                                v_now[0:KR, kt, h].rearrange("p a b -> p (a b)"),
                                start=(kt == 0 and part is ph), stop=(kt == KT - 1 and part is pl))
                last.then_inc(pv_done, 1)

            def turn(rows, bank, src, size=P):
                for c in range(DC):
                    last = pe.transpose(ps_fill[:, bank, c * size:(c + 1) * size],
                                        src[0:rows, c * P:(c + 1) * P], ident[0:rows, 0:rows])
                return last

            def fill(kind, i, b, bank):
                n, p_ = b + 1, b - 1
                if kind == "cx":
                    pe.wait_ge(ctx_normed, (b + 2) * 6 + (i + 1))
                    last = turn(KR, bank, ctx_raw[:, i, :], KR)
                elif kind == "xx":
                    pe.wait_ge(x_normed, (b + 2) * 2 + (i + 1))
                    last = turn(P, bank, xq[:, i, :])
                elif kind == "q":
                    if i == 0:
                        pe.wait_ge(x_split, n * 2 + 2)
                        if isinstance(b, int) and b == -1:
                            pe.wait_ge(w_split, DC)
                    for j in range(2):
                        m = slice((2 * i + j) * P, (2 * i + j + 1) * P)
                        last = three(ps_fill[:, bank, j * NQ:(j + 1) * NQ],
                                     lambda a, c: whl["q"][a][:, c, m], lambda a, c: x_t[a][:, c, :])
                elif kind == "k":
                    if i == 0:
                        pe.wait_ge(ctx_split, n * 6 + 6)
                        if isinstance(b, int) and b == -1:
                            pe.wait_ge(w_split, 2 * DC)
                    m, r = slice((i // 2) * P, (i // 2 + 1) * P), slice((i % 2) * KH, (i % 2 + 1) * KH)
                    last = three(ps_fill[:, bank, 0:KH], lambda a, c: whl["k"][a][:, c, m],
                                 lambda a, c: ctx_t[a][:, c, r])
                elif kind == "v":
                    if i == 0 and isinstance(b, int) and b == -1:
                        pe.wait_ge(w_split, 3 * DC)
                    r = slice(i * KR, (i + 1) * KR)
                    last = three(ps_fill[0:KR, bank, :], lambda a, c: ctx_t[a][:, c, r],
                                 lambda a, c: whl["v"][a][:, c, :])
                elif kind == "mr":
                    m, nb = (i, b) if i > 0 else (0, n)
                    pe.wait_ge(max_split, nb * 8 + (m + 1))
                    for h in (2 * m, 2 * m + 1):
                        for t in range(2):
                            frm, to = q_cols(t)
                            last = pe.matmul(
                                ps_fill[SPLIT_ROWS:MAX_END, bank, (h % 2) * NQ + to.start:(h % 2) * NQ + to.stop],
                                mhl[:, h, t, :], ident16[:, frm], start=True, stop=True,
                                tile_position=(0, SPLIT_ROWS))
                elif kind == "ot":
                    pe.wait_ge(o_normed, p_ * 2 + (i + 1))
                    last = turn(P, bank, yo[:, i, :])
                elif kind == "op":
                    if i == 0:
                        pe.wait_ge(o_split, p_ * 2 + 2)
                    last = three(ps_fill[:, bank, :], lambda a, c: o_t[a][:, c, QSTART[i]:QSTART[i] + P],
                                 lambda a, c: whl["o"][a][:, c, :])
                elif kind == "yt":
                    pe.wait_ge(y_normed, p_ * 2 + (i + 1))
                    last = turn(P, bank, yo[:, i, :])
                elif kind == "f1":
                    if i == 0:
                        wait_alone(pe, y_split, p_ * 2 + 2)
                        if not isinstance(b, int):
                            pe.wait_ge(piece_done, PIECES)
                    for j in range(2):
                        m = slice((2 * i + j) * P, (2 * i + j + 1) * P)
                        last = three(ps_fill[:, bank, j * NQ:(j + 1) * NQ], lambda a, c: w1q[:, c, m],
                                     lambda a, c: o_t[a][:, c, :], order=((0, 0), (0, 1)))
                else:
                    def ready(c):
                        if c % 2 == 0:
                            pe.wait_ge(h_split, p_ * 8 + (c // 2 + 1))
                    if i == 0 and not isinstance(b, int):
                        wait_alone(pe, h_split, p_ * 8 + 8)
                    t, w = i // 2, slice((i % 2) * 256, (i % 2 + 1) * 256)
                    r = slice(QSTART[t], QSTART[t] + P)
                    last = three(ps_fill[:, bank, 0:256], lambda a, c: (hh, hl)[a][:, c, r],
                                 lambda a, c: w2q[:, c, w], order=((0, 0), (1, 0)), chunks=FC,
                                 ready=ready if i == 0 and isinstance(b, int) else None)
                last.then_inc(fill_ready, 1)

            def bias_sum(j):
                name, beta = (("q", 16), ("k", 24), ("v", 24))[j]
                if j == 0:
                    pe.wait_ge(small_loaded, 80)
                pe.wait_ge(w_loaded[name], 16)
                for c in range(DC):
                    last = pe.matmul(ps_bias[j], col[:, beta + c:beta + c + 1], raw[name][:, c, :],
                                     start=(c == 0), stop=(c == DC - 1))
                last.then_inc(bias_sums, 1)

            def bo_sum():
                pe.wait_ge(wide_ready, DC)
                for c in range(DC):
                    last = pe.matmul(ps_pv[:, 1, :], bv_wide[:, c, :], raw["o"][:, c, :],
                                     start=(c == 0), stop=(c == DC - 1))
                last.then_inc(bo_sums, 1)

            def threshold():
                pe.wait_ge(tot_ready, 2)
                pe.matmul(ps_pv[:, 0, 0:2], ones[:, :], abs_tot[:, :], start=True, stop=True).then_inc(tot_all, 1)

            def before(stages):
                return ORDER[ORDER.index(stages) - 1]

            def body(b, stages):
                done = []
                if stages != OPEN:
                    last_two = fill_list(before(stages))[-2:] + (fill_list(INNER)[-2:] if stages == INNER else [])
                    for s, value in {freed(*f, b - 1)[0].name: freed(*f, b - 1) for f in last_two}.values():
                        pe.wait_ge(s, value)
                for slot in range(H):
                    for kind, i in slot_steps(slot, *stages):
                        if kind == "score":
                            h = (slot + 4) % H
                            score(b + 1 if slot >= 12 else b, h, i)
                        elif kind == "expo":
                            expo(b, slot, i)
                        elif kind == "pv":
                            pv(b if slot else b - 1, i)
                        elif kind == "bias_sum":
                            bias_sum(i)
                        elif kind == "bo_sum":
                            bo_sum()
                        elif kind == "threshold":
                            threshold()
                        elif kind in FILL_KINDS:
                            if len(done) >= 2:
                                if kind in ("f1", "f2"):
                                    wait_alone(pe, *freed(*done[-2], b))
                                else:
                                    pe.wait_ge(*freed(*done[-2], b))
                            fill(kind, i, b, len(done) % 2)
                            done.append((kind, i))

            pe.wait_ge(consts, 5)
            body(-2, OPEN)
            body(-1, FIRST)
            pe.wait_ge(thr_step, 1)
            pe.wait_ge(bo_step, 2)
            pe.wait_ge(rows_set, 16 * (STACK_ROWS - SPLIT_ROWS))
            iterations(pe, body)

        @block.scalar
        def _(act):
            def expo(b, h, u):
                k = 3 * h + u
                act.wait_ge(logits_ready, b * 48 + (k + 1))
                if not (isinstance(b, int) and b * 48 + k < 2):
                    act.wait_ge(p_split, b * 48 + (k - 1))
                if u == 0 and not (isinstance(b, int) and b * 16 + h < 2):
                    act.wait_ge(pv_done, b * 16 + (h - 1))
                unit = 3 * (h % 2) + u
                nc.scalar.activation(p_full[0:KR, k % 2, :], ps_exp[0:KR, k % 2, 0:2 * NQ], ACT.Exp,
                                     scale=EXP_SCALE)
                nc.scalar.activation(ph[0:KR, unit, :], ps_exp[0:KR, k % 2, 0:2 * NQ], ACT.Exp,
                                     scale=EXP_SCALE).then_inc(exp_done, 1)

            def fill(kind, i, b, bank, ready):
                n, p_ = b + 1, b - 1
                if kind in ("op", "f2"):
                    return
                act.wait_ge(fill_ready, ready)
                if kind == "cx":
                    nc.scalar.activation(ctx_t[0][:, :, i * KR:(i + 1) * KR],
                                         ps_fill[:, bank, 0:DC * KR].rearrange("p (c n) -> p c n", c=DC),
                                         ACT.Copy, scale=Z_SCALE).then_inc(ctx_hi, 1)
                elif kind in ("xx", "ot", "yt"):
                    dst, scale, s = {"xx": (x_t, Z_SCALE, x_hi), "ot": (o_t, 1.0, o_hi),
                                     "yt": (o_t, Y_SCALE, y_hi)}[kind]
                    frm, to = q_cols(i)
                    src = ps_fill[:, bank, :].rearrange("p (c n) -> p c n", c=DC)[:, :, frm]
                    nc.scalar.activation(dst[0][:, :, to], src, ACT.Copy, scale=scale).then_inc(s, 1)
                elif kind == "q":
                    if isinstance(b, int) and b == -1 and i == 0:
                        act.wait_ge(bias_step, 3)
                    if not (isinstance(b, int) and b == -1):
                        act.wait_ge(qk_split, n * 10 + (i - 1))
                    for j in range(2):
                        last = nc.scalar.activation(qk_full[:, i % 2, j * NQ:(j + 1) * NQ],
                                                    ps_fill[:, bank, j * NQ:(j + 1) * NQ], ACT.Identity,
                                                    bias=bias4[:, 2 * i + j:2 * i + j + 1], scale=PSUM_TO_QK)
                    last.then_inc(qk_lifted, 1)
                elif kind == "k":
                    act.wait_ge(qk_split, n * 10 + (i + 1))
                    nc.scalar.activation(qk_full[:, i % 2, 0:KH], ps_fill[:, bank, 0:KH], ACT.Identity,
                                         bias=bias4[:, 4 + i // 2:5 + i // 2],
                                         scale=PSUM_TO_QK).then_inc(qk_lifted, 1)
                elif kind == "v":
                    if i == 0 and not (isinstance(b, int) and b == -1):
                        act.wait_ge(v_landed[3], n * 16)
                    nc.scalar.activation(v_stage[0:KR, i, :, 0, 0:HD],
                                         ps_fill[0:KR, bank, :].rearrange("p (h d) -> p h d", h=H),
                                         ACT.Copy, scale=PSUM_TO_V).then_inc(v_hi, 1)
                elif kind == "mr":
                    m = max(i, 0)
                    nc.scalar.activation(q_stack[SPLIT_ROWS:MAX_END, 2 * m:2 * m + 2, :],
                                         ps_fill[SPLIT_ROWS:MAX_END, bank, 0:2 * NQ]
                                         .rearrange("p (h n) -> p h n", h=2), ACT.Copy).then_inc(shift_rows, 1)
                elif kind == "f1":
                    if i >= 2:
                        act.wait_ge(h_split, p_ * 8 + (i - 1))
                    for j in range(2):
                        last = nc.scalar.activation(h_full[:, i % 2, j * NQ:(j + 1) * NQ],
                                                    ps_fill[:, bank, j * NQ:(j + 1) * NQ], ACT.Relu,
                                                    bias=b1y[:, 2 * i + j:2 * i + j + 1])
                    last.then_inc(h_lifted, 1)

            def norm(n, j):
                if j == 0:
                    act.wait_ge(norm1_ready, n + 1)
                if j < KT:
                    nc.scalar.activation(ctx_raw[0:KR, j, :], ctx_raw[0:KR, j, :], ACT.Identity,
                                         bias=r1[0:KR, 4, j:j + 1], scale=r1[0:KR, 3, j:j + 1]) \
                        .then_inc(ctx_normed, 1)
                else:
                    nc.scalar.activation(xq[:, j - KT, :], xq[:, j - KT, :], ACT.Identity,
                                         bias=r1[:, 4, j:j + 1], scale=r1[:, 3, j:j + 1]) \
                        .then_inc(x_normed, 1)

            def norm2(p_, t):
                if t == 0:
                    act.wait_ge(norm2_ready, p_ + 1)
                    act.wait_ge(o_split, p_ * 2 + 2)
                nc.scalar.activation(yo[:, t, :], xb[:, t, :], ACT.Identity, bias=r2[:, 4, t:t + 1],
                                     scale=r2[:, 3, t:t + 1]).then_inc(y_normed, 1)

            def weight_hi(k):
                name, at = (("q", 0), ("k", 4), ("v", 4), ("o", 8))[k // DC]
                c = k % DC
                if k == 0:
                    act.wait_ge(gains_ready, 4)
                if c == 0:
                    act.wait_ge(w_loaded[name], 16)
                at += 0 if name == "o" else c
                nc.scalar.activation(whl[name][0][:, c, :], raw[name][:, c, :], ACT.Copy,
                                     scale=gains[:, at:at + 1]).then_inc(w_hi, 1)

            def sum_piece(k):
                act.wait_ge(piece_loaded[k % PIECE_RING], 16 * (k // PIECE_RING + 1))
                nc.scalar.activation(piece[:, k % PIECE_RING, :], piece[:, k % PIECE_RING, :], ACT.Abs,
                                     accum_out=abs_sum[:, k:k + 1]).then_inc(piece_summed, 1)
                act.wait_ge(piece_summed, k + 1)
                load_piece(act, k + PIECE_RING)

            def body(b, stages):
                done = 0
                for slot in range(H):
                    for kind, i in slot_steps(slot, *stages):
                        if kind == "expo":
                            expo(b, slot, i)
                        elif kind == "norm":
                            norm(b + 2, i)
                        elif kind == "weight":
                            weight_hi(i)
                        elif kind == "load_pieces":
                            act.wait_ge(w_loaded["v"], 16)
                            for k in range(PIECE_RING):
                                load_piece(act, k)
                        elif kind == "piece_sum":
                            sum_piece(i)
                        elif kind == "reload":
                            act.wait_ge(piece_compared, i + 1)
                            load_piece(act, PIECES + i + PIECE_RING)
                        elif kind == "norm2":
                            norm2(b - 1, i)
                        elif kind in FILL_KINDS:
                            fill(kind, i, b, done % 2, fills_before(b) + (done + 1))
                            done += 1

            act.wait_ge(consts, 8)
            act.wait_ge(small_loaded, 80)
            nc.scalar.activation(gt[:, :], g2[:, :], ACT.Tanh).then_inc(gate_ready, 1)
            body(-2, OPEN)
            body(-1, FIRST)
            act.wait_ge(w_split, 4 * DC)
            act.wait_ge(bo_sums, 1)
            iterations(act, body)

        @block.vector
        def _(dve):
            def score(n, h, t):
                dve.wait_ge(scores_ready, n * 32 + (2 * h + t + 1))
                nc.vector.tensor_reduce(mx[:, h, t:t + 1], ps_score[:, :, 0:KH], AX.XY, ALU.max) \
                    .then_inc(max_taken, 1)

            def split_max(n, m):
                dve.wait_ge(max_taken, n * 32 + (4 * m + 4))
                nc.vector.tensor_scalar(mhl[:, 2 * m:2 * m + 2, :, 0], mx[:, 2 * m:2 * m + 2, :], 1.0 / M_SCALE,
                                        None, ALU.mult).then_inc(max_hi, 1)
                dve.wait_ge(max_hi, n * 8 + (m + 1))
                nc.vector.scalar_tensor_tensor(mhl[:, 2 * m:2 * m + 2, :, 1], mx[:, 2 * m:2 * m + 2, :],
                                               1.0 / M_SCALE, mhl[:, 2 * m:2 * m + 2, :, 0],
                                               ALU.mult, ALU.subtract).then_inc(max_split, 1)

            def expo(b, h, u):
                k, unit = 3 * h + u, 3 * (h % 2) + u
                dve.wait_ge(exp_done, b * 48 + (k + 1))
                nc.vector.tensor_tensor(pl[0:KR, unit, :], p_full[0:KR, k % 2, :], ph[0:KR, unit, :],
                                        ALU.subtract).then_inc(p_split, 1)

            def take_o(b, h):
                dve.wait_ge(pv_done, b * 16 + (h + 1))
                if h == 0 and not (isinstance(b, int) and b == 0):
                    dve.wait_ge(o_normed, b * 2)
                nc.vector.tensor_reduce(o_sum[:, :, h, :],
                                        ps_pv[:, h % 2, 0:4 * VW].rearrange("p (t s d) -> p t d s", t=2, s=2),
                                        AX.X, ALU.add).then_inc(o_taken, 1)

            def divide(b):
                dve.wait_ge(o_taken, b * 16 + 16)
                nc.vector.reciprocal(rden[:, :, :], o_sum[:, :, :, HD]).then_inc(o_recip, 1)
                dve.wait_ge(o_recip, b + 1)
                for t in range(2):
                    nc.vector.tensor_tensor(yo[:, t, :].rearrange("p (h d) -> p h d", h=H),
                                            o_sum[:, t, :, 0:HD],
                                            rden[:, t, :].unsqueeze(2).to_broadcast([P, H, HD]),
                                            ALU.mult).then_inc(o_normed, 1)

            def stat(n, j):
                if j == 0:
                    dve.wait_ge(ctx_loaded, n * 16 + 16)
                if j == KT:
                    dve.wait_ge(x_loaded, n * 32 + 32)
                if j < KT:
                    nc.vector.bn_stats(bn1[0:KR, j, :], ctx_raw[0:KR, j, :]).then_inc(stats1_step, 1)
                else:
                    nc.vector.bn_stats(bn1[:, j, :], xq[:, j - KT, :]).then_inc(stats1_step, 1)
                if j == KT + 1:
                    if not (isinstance(n, int) and n == 0):
                        wait_alone(dve, x_normed, n * 2)
                    wait_alone(dve, stats1_step, n * 8 + 8)
                    for i in range(KT):
                        nc.vector.bn_aggr(mv1[0:KR, i, :], bn1[0:KR, i, :])
                    for i in range(KT, KT + 2):
                        last = nc.vector.bn_aggr(mv1[:, i, :], bn1[:, i, :])
                    last.then_inc(stats1, 1)

            def stats_finish(p_):
                for t in range(2):
                    dve.wait_ge(x1_ready, p_ * 2 + (t + 1))
                    last = nc.vector.bn_stats(bn2[:, t, :], xb[:, t, :])
                last.then_inc(stats2_step, 1)
                wait_alone(dve, stats2_step, p_ + 1)
                for t in range(2):
                    last = nc.vector.bn_aggr(mv2[:, t, :], bn2[:, t, :])
                last.then_inc(stats2, 1)

            def fill(kind, i, b, bank, ready):
                n, p_ = b + 1, b - 1
                if kind == "cx":
                    dve.wait_ge(ctx_hi, (b + 2) * 6 + (i + 1))
                    r = slice(i * KR, (i + 1) * KR)
                    nc.vector.scalar_tensor_tensor(
                        ctx_t[1][:, :, r], ps_fill[:, bank, 0:DC * KR].rearrange("p (c n) -> p c n", c=DC),
                        Z_SCALE, ctx_t[0][:, :, r], ALU.mult, ALU.subtract).then_inc(ctx_split, 1)
                elif kind in ("xx", "ot", "yt"):
                    dst, scale, hi, s = {"xx": (x_t, Z_SCALE, x_hi, x_split), "ot": (o_t, 1.0, o_hi, o_split),
                                         "yt": (o_t, Y_SCALE, y_hi, y_split)}[kind]
                    dve.wait_ge(hi, (b + 2 if kind == "xx" else p_) * 2 + (i + 1))
                    frm, to = q_cols(i)
                    src = ps_fill[:, bank, :].rearrange("p (c n) -> p c n", c=DC)[:, :, frm]
                    nc.vector.scalar_tensor_tensor(dst[1][:, :, to], src, scale, dst[0][:, :, to],
                                                   ALU.mult, ALU.subtract).then_inc(s, 1)
                elif kind == "q":
                    if i == 0 and not (isinstance(b, int) and b == -1):
                        for g in range(4):
                            dve.wait_ge(kq_landed[g], n * 96)
                    dve.wait_ge(qk_lifted, n * 10 + (i + 1))
                    nc.vector.tensor_copy(qh[:, 2 * i:2 * i + 2, :],
                                          qk_full[:, i % 2, 0:2 * NQ].rearrange("p (c n) -> p c n", c=2)) \
                        .then_inc(qk_hi, 1)
                elif kind == "k":
                    dve.wait_ge(qk_lifted, n * 10 + (i + 3))
                    nc.vector.tensor_copy(kh[:, i // 2, (i % 2) * KH:(i % 2 + 1) * KH],
                                          qk_full[:, i % 2, 0:KH]).then_inc(qk_hi, 1)
                elif kind == "v":
                    dve.wait_ge(v_hi, n * 6 + (i + 1))
                    nc.vector.scalar_tensor_tensor(
                        v_stage[0:KR, i, :, 1, 0:HD], ps_fill[0:KR, bank, :].rearrange("p (h d) -> p h d", h=H),
                        PSUM_TO_V, v_stage[0:KR, i, :, 0, 0:HD], ALU.mult, ALU.subtract).then_inc(v_split, 1)
                elif kind == "op":
                    dve.wait_ge(fill_ready, ready)
                    dve.wait_ge(xb_biased, p_ * 2 + (i + 1))
                    nc.vector.scalar_tensor_tensor(xb[:, i, :], ps_fill[:, bank, :], PSUM_TO_O, xb[:, i, :],
                                                   ALU.mult, ALU.add).then_inc(x1_ready, 1)
                    if i == 1:
                        stats_finish(p_)
                elif kind == "f1":
                    dve.wait_ge(h_lifted, p_ * 8 + (i + 1))
                    nc.vector.tensor_copy(hh[:, 2 * i:2 * i + 2, :],
                                          h_full[:, i % 2, :].rearrange("p (c n) -> p c n", c=2)) \
                        .then_inc(h_hi, 1)
                elif kind == "f2":
                    dve.wait_ge(fill_ready, ready)
                    dve.wait_ge(x1_biased, p_ * 2 + (i // 2 + 1))
                    w = slice((i % 2) * 256, (i % 2 + 1) * 256)
                    nc.vector.scalar_tensor_tensor(xb[:, i // 2, w], ps_fill[:, bank, 0:256], gains[:, 9:10],
                                                   xb[:, i // 2, w], ALU.mult, ALU.add).then_inc(out_ready, 1)

            def gain():
                dve.wait_ge(small_loaded, 80)
                nc.vector.tensor_scalar(gains[:, 0:4], col[:, 12:16], W_SCALE, None, ALU.mult).then_inc(gains_ready, 1)
                nc.vector.tensor_scalar(gains[:, 4:8], col[:, 20:24], W_SCALE, None, ALU.mult).then_inc(gains_ready, 1)
                dve.wait_ge(gate_ready, 1)
                nc.vector.tensor_scalar(gains[:, 8:9], gt[:, 0:1], W_SCALE, None, ALU.mult).then_inc(gains_ready, 1)
                nc.vector.tensor_scalar(gains[:, 9:10], gt[:, 1:2], 1.0 / Y_SCALE, None, ALU.mult) \
                    .then_inc(gains_ready, 1)
                nc.vector.tensor_scalar(b1y[:, :], col[:, 28:44], Y_SCALE, None, ALU.mult)
                nc.vector.tensor_scalar(b2_row[:, :], b2_row[:, :], gt[:, 1:2], None, ALU.mult).then_inc(bo_step, 1)
                dve.wait_ge(gains_ready, 4)

            def weight_lo(k):
                name, at = (("q", 0), ("k", 4), ("v", 4), ("o", 8))[k // DC]
                c = k % DC
                at += 0 if name == "o" else c
                dve.wait_ge(w_hi, k + 1)
                nc.vector.scalar_tensor_tensor(whl[name][1][:, c, :], raw[name][:, c, :], gains[:, at:at + 1],
                                               whl[name][0][:, c, :], ALU.mult, ALU.subtract).then_inc(w_split, 1)

            def bias_row(j):
                dve.wait_ge(bias_sums, j + 1)
                nc.vector.tensor_copy(bias_rows.rearrange("o (p j c) -> o j c p", p=P, j=3)[:, j],
                                      ps_bias[j].rearrange("o (c p) -> o c p", c=DC)).then_inc(bias_row_ready, 1)

            def bias_ready():
                dve.wait_ge(bias_turned, 16)
                nc.vector.tensor_tensor(bias[:, :], bias[:, :], col[:, 0:12], ALU.add).then_inc(bias_step, 1)
                dve.wait_ge(bias_step, 1)
                nc.vector.tensor_scalar(bias4[:, :], bias[:, 0:8], QK_SCALE, None, ALU.mult).then_inc(bias_step, 2)
                for c in range(DC):
                    nc.vector.tensor_scalar(bv_wide[:, c, :], ones[:, :], bias[:, 8 + c:9 + c], None,
                                            ALU.mult).then_inc(wide_ready, 1)

            def tot():
                dve.wait_ge(piece_summed, PIECES)
                for j in range(2):
                    nc.vector.tensor_reduce(abs_tot[:, j:j + 1], abs_sum[:, 8 * j:8 * j + 8], AX.X, ALU.add) \
                        .then_inc(tot_ready, 1)

            def bo_ready():
                dve.wait_ge(bo_sums, 1)
                nc.vector.tensor_tensor(bo_row[:, :], ps_pv[:, 1, :], bo_row[:, :], ALU.add).then_inc(bo_step, 1)
                dve.wait_ge(bo_step, 2)
                nc.vector.tensor_scalar(bo_row[:, :], bo_row[:, :], gt[:, 0:1], None, ALU.mult).then_inc(bo_step, 1)

            def threshold():
                dve.wait_ge(tot_all, 1)
                nc.vector.tensor_scalar(thr[:, 0:2], ps_pv[:, 0, 0:2], 0.5 / (D * F), 0.5 * EPS, ALU.mult, ALU.add) \
                    .then_inc(thr_step, 1)
                dve.wait_ge(thr_step, 1)
                nc.vector.tensor_scalar(thr[:, 2:4], thr[:, 0:2], -1.0, None, ALU.mult).then_inc(thr_step, 1)

            def compare(k):
                j, kk = k // 8, PIECES + k
                dve.wait_ge(piece_loaded[kk % PIECE_RING], 16 * (kk // PIECE_RING + 1))
                if k == 0:
                    dve.wait_ge(thr_step, 2)
                else:
                    dve.wait_ge(piece_done, k)
                nc.vector.tensor_scalar(above, piece[:, kk % PIECE_RING, :], thr[:, j:j + 1], None, ALU.is_gt)
                nc.vector.tensor_scalar(below, piece[:, kk % PIECE_RING, :], thr[:, 2 + j:3 + j], None, ALU.is_lt) \
                    .then_inc(piece_compared, 1)

            def body(b, stages):
                done = 0
                attend, prep, finish, norm = stages
                for slot in range(H):
                    m = slot // 2 + 1
                    if slot % 2 == 0 and (prep if m == H // 2 else attend):
                        split_max(b if m < H // 2 else b + 1, m % (H // 2))
                    for kind, i in slot_steps(slot, *stages):
                        if kind == "score":
                            score(b + 1 if slot >= 12 else b, (slot + 4) % H, i)
                        elif kind == "expo":
                            if i:
                                expo(b, slot, i - 1)
                            elif slot:
                                expo(b, slot - 1, 2)
                            elif stages != SECOND:
                                expo(b - 1, H - 1, 2)
                        elif kind == "pv":
                            take_o(b if slot else b - 1, i)
                        elif kind == "stat":
                            stat(b + 2, i)
                        elif kind == "gain":
                            gain()
                        elif kind == "weight":
                            weight_lo(i)
                        elif kind == "bias_sum":
                            bias_row(i)
                        elif kind == "tot":
                            tot()
                        elif kind == "bo_sum":
                            bo_ready()
                        elif kind == "threshold":
                            threshold()
                        elif kind == "bias_ready":
                            bias_ready()
                        elif kind == "ternary":
                            compare(i)
                        elif kind == "divide":
                            divide(b - 1)
                        elif kind in FILL_KINDS:
                            fill(kind, i, b, done % 2, fills_before(b) + (done + 1))
                            done += 1
                if stages == SECOND:
                    dve.wait_ge(piece_done, PIECES)
                if stages == SECOND_LAST:
                    expo(b, H - 1, 2)

            dve.wait_ge(consts, 5)
            nc.vector.memset(thr[:, :], 0.0).then_inc(out_ready, 4)
            body(-2, OPEN)
            body(-1, FIRST)
            dve.wait_ge(thr_step, 2)
            iterations(dve, body)

        @block.gpsimd
        def _(pool):
            def rstd(r, step, base, width, mean, done):
                nc.gpsimd.tensor_tensor(r[:, 1, :], r[:, 0, :], minus_half[:, 0:width], ALU.pow).then_inc(step, 1)
                pool.wait_ge(step, base + 1)
                nc.gpsimd.tensor_tensor(r[:, 2, :], r[:, 1, :], r[:, 1, :], ALU.mult).then_inc(step, 1)
                pool.wait_ge(step, base + 2)
                nc.gpsimd.tensor_tensor(r[:, 2, :], r[:, 2, :], r[:, 0, :], ALU.mult).then_inc(step, 1)
                wait_alone(pool, step, base + 3)
                nc.gpsimd.tensor_scalar(r[:, 2, :], r[:, 2, :], -0.5, 1.5, ALU.mult, ALU.add).then_inc(step, 1)
                pool.wait_ge(step, base + 4)
                nc.gpsimd.tensor_tensor(r[:, 3, :], r[:, 1, :], r[:, 2, :], ALU.mult).then_inc(step, 1)
                pool.wait_ge(step, base + 5)
                nc.gpsimd.tensor_tensor(r[:, 4, :], mean, r[:, 3, :], ALU.mult).then_inc(step, 1)
                wait_alone(pool, step, base + 6)
                nc.gpsimd.tensor_scalar(r[:, 4, :], r[:, 4, :], -1.0, None, ALU.mult).then_inc(done, 1)

            def rstd_prep(n):
                wait_alone(pool, stats1, n + 1)
                nc.gpsimd.tensor_scalar(r1[:, 0, 0:KT], mv1[:, 0:KT, 1], EPS, None, ALU.add).then_inc(rstd1_step, 1)
                nc.gpsimd.tensor_scalar(r1[:, 0, KT:8], mv1[:, KT:8, 1], 1.0 + EPS, EPS * EPS, ALU.mult, ALU.add) \
                    .then_inc(rstd1_step, 1)
                pool.wait_ge(rstd1_step, n * 8 + 2)
                rstd(r1, rstd1_step, n * 8 + 2, 8, mv1[:, :, 0], norm1_ready)

            def rstd_finish(p_):
                wait_alone(pool, stats2, p_ + 1)
                nc.gpsimd.tensor_scalar(r2[:, 0, :], mv2[:, :, 1], EPS, None, ALU.add).then_inc(rstd2_step, 1)
                pool.wait_ge(rstd2_step, p_ * 7 + 1)
                rstd(r2, rstd2_step, p_ * 7 + 1, 2, mv2[:, :, 0], norm2_ready)

            def bias_x1(p_):
                pool.wait_ge(y_normed, p_ * 2 + 2)
                for t in range(2):
                    nc.gpsimd.tensor_tensor(xb[:, t, :], xb[:, t, :], b2_row[:, :], ALU.add).then_inc(x1_biased, 1)

            def bias_residual(p_):
                pool.wait_ge(xb_loaded, p_ * 32 + 32)
                for t in range(2):
                    nc.gpsimd.tensor_tensor(xb[:, t, :], xb[:, t, :], bo_row[:, :], ALU.add).then_inc(xb_biased, 1)

            def fill(kind, i, b):
                n, p_ = b + 1, b - 1
                if kind == "q":
                    pool.wait_ge(qk_hi, n * 10 + (i + 1))
                    nc.gpsimd.tensor_tensor(ql[:, 2 * i:2 * i + 2, :],
                                            qk_full[:, i % 2, 0:2 * NQ].rearrange("p (c n) -> p c n", c=2),
                                            qh[:, 2 * i:2 * i + 2, :], ALU.subtract).then_inc(qk_split, 1)
                elif kind == "k":
                    pool.wait_ge(qk_hi, n * 10 + (i + 3))
                    r = slice((i % 2) * KH, (i % 2 + 1) * KH)
                    nc.gpsimd.tensor_tensor(kl[:, i // 2, r], qk_full[:, i % 2, 0:KH], kh[:, i // 2, r],
                                            ALU.subtract).then_inc(qk_split, 1)
                elif kind == "f1":
                    pool.wait_ge(h_hi, p_ * 8 + (i + 1))
                    nc.gpsimd.tensor_tensor(hl[:, 2 * i:2 * i + 2, :],
                                            h_full[:, i % 2, :].rearrange("p (c n) -> p c n", c=2),
                                            hh[:, 2 * i:2 * i + 2, :], ALU.subtract).then_inc(h_split, 1)

            def ternary(k):
                dst = w1q[:, k // 2, (k % 2) * 1024:(k % 2 + 1) * 1024] if k < 8 else \
                    w2q[:, 2 * (k - 8):2 * (k - 8) + 2, :].rearrange("p c n -> p (c n)")
                pool.wait_ge(piece_compared, k + 1)
                nc.gpsimd.tensor_tensor(dst, above, below, ALU.subtract, saturate=False).then_inc(piece_done, 1)

            def body(b, stages):
                for slot in range(H):
                    for kind, i in slot_steps(slot, *stages):
                        if kind == "ternary":
                            ternary(i)
                        elif kind == "bias":
                            bias_residual(b - 1)
                        elif kind == "rstd":
                            rstd_prep(b + 2)
                        elif kind == "rstd2":
                            rstd_finish(b - 1)
                        elif kind == "bias2":
                            bias_x1(b - 1)
                        else:
                            fill(kind, i, b)

            nc.gpsimd.memset(ident[:, :], 0.0).then_inc(consts, 1)
            pool.wait_ge(consts, 1)
            nc.gpsimd.affine_select(out=ident[:, :], in_=ident[:, :], compare_op=ALU.not_equal, fill=1.0,
                                    base=0, pattern=[[-1, P]], channel_multiplier=1).then_inc(consts, 1)
            pool.wait_ge(consts, 2)
            nc.gpsimd.tensor_copy(ident16[:, :], ident[:, :]).then_inc(consts, 1)
            nc.gpsimd.memset(ones[:, :], 1.0).then_inc(consts, 1)
            nc.gpsimd.memset(minus_half[:, :], -0.5)
            nc.gpsimd.memset(mv1[:, :, :], 1.0)
            nc.gpsimd.memset(v_stage[:, :, :, :, HD:VW], 0.0).then_inc(consts, 1)
            pool.wait_ge(consts, 5)
            nc.gpsimd.memset(v_stage[:, :, :, 0, HD:VW], 1.0).then_inc(consts, 1)
            nc.gpsimd.memset(minus_m[:, :], -M_SCALE).then_inc(consts, 1)
            pool.wait_ge(consts, 7)
            nc.gpsimd.memset(q_stack[SPLIT_ROWS:STACK_ROWS, :, :], -SHIFT).then_inc(consts, 1)
            pool.wait_ge(consts, 8)
            body(-2, OPEN)
            body(-1, FIRST)
            pool.wait_ge(bo_step, 3)
            iterations(pool, body)


def kernel(**inputs):
    import numpy as _np
    import concourse.bacc as _bacc
    from concourse import mybir as _mybir
    from concourse.bass_utils import run_bass_kernel_spmd as _run

    a = {k: _np.asarray(v) for k, v in inputs.items()}
    pre = "L0_xattn_"
    order = _np.arange(512).reshape(4, 4, 32).transpose(1, 0, 2).ravel()
    a[pre + "Wv"], a[pre + "bv"] = a[pre + "Wv"][:, order], a[pre + "bv"][order]
    a[pre + "Wo"] = a[pre + "Wo"][order]
    cols = [a[pre + n].reshape(-1, 128).T for n in ("bq", "bk", "bv", "gq", "betq", "gkv", "betkv")]
    cols.append(a["L0_ffn_b1"].reshape(-1, 128).T)
    arrays = {
        "x": a["x"], "ctx_in": a["ctx_1024"],
        "w_q": a[pre + "Wq"], "w_k": a[pre + "Wk"], "w_v": a[pre + "Wv"], "w_o": a[pre + "Wo"],
        "w1t": a["L0_ffn_W1"].T, "w2t": a["L0_ffn_W2"].T,
        "cols": _np.concatenate(cols, axis=1),
        "bo": a[pre + "bo"], "b2": a["L0_ffn_b2"], "g_x": a["g_xattn"], "g_f": a["g_ffn"],
    }
    arrays = {k: _np.ascontiguousarray(v) for k, v in arrays.items()}
    nc = _bacc.Bacc("TRN2", target_bir_lowering=False, num_devices=1)
    args = {k: nc.dram_tensor(k, v.shape, _mybir.dt.from_np(v.dtype), kind="ExternalInput").ap()
            for k, v in arrays.items()}
    out = nc.dram_tensor("out", a["x"].shape, _mybir.dt.float32, kind="ExternalOutput").ap()
    gated_block(nc, out=out, **args)
    r = _run(nc, [arrays], core_ids=[0])
    return r.results[0]["out"]
```
